# Optimizing a Trainium2 kernel written in Bass

```python
import numpy as np
import jax
import jax.numpy as jnp

def _softmax(x, axis=-1):
    return jax.nn.softmax(x, axis=axis)

def _gelu(x):
    return jax.nn.gelu(x, approximate=True)

def _silu(x):
    return jax.nn.silu(x)

def _sigmoid(x):
    return jax.nn.sigmoid(x)

def _layernorm(x, axis=-1, eps=1e-05):
    m = jnp.mean(x, axis=axis, keepdims=True)
    v = jnp.var(x, axis=axis, keepdims=True)
    return (x - m) / jnp.sqrt(v + eps)

def _scatter_add(tgt, idx, src, axis=0):
    return tgt.at[idx].add(src)

def _segment_sum(src, seg, n):
    return jax.ops.segment_sum(src, seg, n)
kernel_name = 'mk_flamingo_gated_d1_seqx_r8_376c1c'

def setup_inputs(seed: int=0):
    np.random.seed(seed)
    _w = jnp.asarray

    def _rec_inputs():
        import jax
        import jax.numpy as jnp
        _rk = jax.random.key(seed)
        x = -0.0002928 + 1 * jax.random.normal(jax.random.fold_in(_rk, 1), (4, 256, 256), jnp.float32)
        _lenS = 256 - jax.random.randint(jax.random.fold_in(_rk, 7), (4,), 0, max(1, 256 // 4) + 1, jnp.int32)
        _lenS2 = 256 - jax.random.randint(jax.random.fold_in(_rk, 8), (4,), 0, max(1, 256 // 4) + 1, jnp.int32)
        _ctx_512P = jax.random.normal(jax.random.fold_in(_rk, 11), (4, 16, 64), jnp.float32)
        _ctx_512c = jax.random.dirichlet(jax.random.fold_in(_rk, 511), 0.3 * jnp.ones((16,), jnp.float32), (4, 256))
        _ctx_512t = jnp.einsum('bsk,bkd->bsd', _ctx_512c, _ctx_512P)
        _ctx_512t = _ctx_512t * jax.lax.rsqrt(jnp.mean(jnp.square(_ctx_512t)) + 1e-12) * 0.953939
        ctx_512 = 0.000227908 + 0.99994 * (_ctx_512t + 0.3 * jax.random.normal(jax.random.fold_in(_rk, 611), (4, 256, 64), jnp.float32))
        _g = jax.random.normal(jax.random.fold_in(_rk, 9001), (2, 1), jnp.float32)
        _g = jnp.sign(_g) * jnp.maximum(jnp.abs(_g), 1.0) + (_g == 0) * 1.0
        g_xattn = _g[0]
        g_ffn = _g[1]
        return (x, ctx_512, g_xattn, g_ffn)
    x, ctx_512, g_xattn, g_ffn = _rec_inputs()

    def _L0_xattn_setup():
        import jax, jax.numpy as jnp
        import numpy as np
        B, S, L = (2, 128, 128)
        DIM_Q, H, K, D_C, D_CQ, R = (256, 16, 128, 64, 192, 64)

        def _rope_tables(seq_len, dim, dtype):
            inv_freq = 1.0 / 10000.0 ** (jnp.arange(0, dim, 2, dtype=dtype) / dim)
            t = jnp.arange(seq_len, dtype=dtype)
            freqs = t[:, None] * inv_freq[None, :]
            sin = jnp.repeat(jnp.sin(freqs), 2, axis=-1)
            cos = jnp.repeat(jnp.cos(freqs), 2, axis=-1)
            return (sin, cos)

        def _rotate_half(x):
            h = x.shape[-1] // 2
            return jnp.concatenate([-x[..., h:], x[..., :h]], axis=-1)
        key = jax.random.key(seed)
        ks = jax.random.split(key, 8)
        s_in = 1.0 / np.sqrt(DIM_Q)
        s_k = 1.0 / np.sqrt(K)
        s_cq = 1.0 / np.sqrt(D_CQ)
        s_c = 1.0 / np.sqrt(D_C)
        return {'hidden_q': jax.random.normal(ks[0], (B, S, DIM_Q), jnp.float32), 'kv_c': jax.random.normal(ks[1], (B, L, D_C), jnp.float32), 'Wq': jax.random.normal(ks[2], (H * K, DIM_Q), jnp.float32) * s_in, 'w_kc_q': jax.random.normal(ks[3], (H, K, D_CQ), jnp.float32) * s_k, 'w_kc_kv': jax.random.normal(ks[4], (H, K, D_C), jnp.float32) * s_k, 'W_qr': jax.random.normal(ks[5], (H, D_CQ, R), jnp.float32) * s_cq / np.sqrt(R), 'W_kr': jax.random.normal(ks[6], (H, D_C, R), jnp.float32) * s_c, 'Wo': jax.random.normal(ks[7], (DIM_Q, H * K), jnp.float32) * s_k}
    _L0_xattn_all = _L0_xattn_setup()
    _L0_xattn_in = {k: v for k, v in _L0_xattn_all.items() if k in ('Wq', 'w_kc_q', 'w_kc_kv', 'W_qr', 'W_kr', 'Wo')}
    del _L0_xattn_all

    def _L0_ffn_setup():
        import jax, jax.numpy as jnp
        import numpy as np
        EPS = 1e-06
        K_STEPS = 4
        USE_GATING = True

        def layer_norm(x, gamma, beta):
            mu = jnp.mean(x, axis=-1, keepdims=True)
            var = jnp.mean(jnp.square(x - mu), axis=-1, keepdims=True)
            return (x - mu) * jax.lax.rsqrt(var + EPS) * gamma + beta
        key = jax.random.key(seed)
        B, L, D, H = (4, 512, 256, 1024)
        ks = jax.random.split(key, 16)
        s = 0.02
        return {'x': jax.random.normal(ks[0], (B, L, D), dtype=jnp.float32), 'in_gamma': jnp.ones((D,), jnp.float32), 'in_beta': jnp.zeros((D,), jnp.float32), 'agg_w': jax.random.normal(ks[1], (D, D), jnp.float32) * s, 'agg_b': jnp.zeros((D,), jnp.float32), 'pn_gamma': jnp.ones((D,), jnp.float32), 'pn_beta': jnp.zeros((D,), jnp.float32), 'd1_w': jax.random.normal(ks[2], (D, H), jnp.float32) * s, 'd1_b': jnp.zeros((H,), jnp.float32), 'd2_w': jax.random.normal(ks[3], (H, D), jnp.float32) * s, 'd2_b': jnp.zeros((D,), jnp.float32), 'bc_w': jax.random.normal(ks[4], (D, D), jnp.float32) * s, 'bc_b': jnp.zeros((D,), jnp.float32), 'gate_w': jax.random.normal(ks[5], (D, D), jnp.float32) * s, 'gate_b': jnp.zeros((D,), jnp.float32), 'out_gamma': jnp.ones((D,), jnp.float32), 'out_beta': jnp.zeros((D,), jnp.float32)}
    _L0_ffn_all = _L0_ffn_setup()
    _L0_ffn_in = {k: v for k, v in _L0_ffn_all.items() if k in ('in_gamma', 'in_beta', 'agg_w', 'agg_b', 'pn_gamma', 'pn_beta', 'd1_w', 'd1_b', 'd2_w', 'd2_b', 'bc_w', 'bc_b', 'gate_w', 'gate_b', 'out_gamma', 'out_beta')}
    del _L0_ffn_all
    return {'x': x, 'ctx_512': ctx_512, 'g_xattn': g_xattn, 'g_ffn': g_ffn, 'L0_xattn_Wq': _L0_xattn_in['Wq'], 'L0_xattn_w_kc_q': _L0_xattn_in['w_kc_q'], 'L0_xattn_w_kc_kv': _L0_xattn_in['w_kc_kv'], 'L0_xattn_W_qr': _L0_xattn_in['W_qr'], 'L0_xattn_W_kr': _L0_xattn_in['W_kr'], 'L0_xattn_Wo': _L0_xattn_in['Wo'], 'L0_ffn_in_gamma': _L0_ffn_in['in_gamma'], 'L0_ffn_in_beta': _L0_ffn_in['in_beta'], 'L0_ffn_agg_w': _L0_ffn_in['agg_w'], 'L0_ffn_agg_b': _L0_ffn_in['agg_b'], 'L0_ffn_pn_gamma': _L0_ffn_in['pn_gamma'], 'L0_ffn_pn_beta': _L0_ffn_in['pn_beta'], 'L0_ffn_d1_w': _L0_ffn_in['d1_w'], 'L0_ffn_d1_b': _L0_ffn_in['d1_b'], 'L0_ffn_d2_w': _L0_ffn_in['d2_w'], 'L0_ffn_d2_b': _L0_ffn_in['d2_b'], 'L0_ffn_bc_w': _L0_ffn_in['bc_w'], 'L0_ffn_bc_b': _L0_ffn_in['bc_b'], 'L0_ffn_gate_w': _L0_ffn_in['gate_w'], 'L0_ffn_gate_b': _L0_ffn_in['gate_b'], 'L0_ffn_out_gamma': _L0_ffn_in['out_gamma'], 'L0_ffn_out_beta': _L0_ffn_in['out_beta']}

def reference(x, ctx_512, g_xattn, g_ffn, L0_xattn_Wq, L0_xattn_w_kc_q, L0_xattn_w_kc_kv, L0_xattn_W_qr, L0_xattn_W_kr, L0_xattn_Wo, L0_ffn_in_gamma, L0_ffn_in_beta, L0_ffn_agg_w, L0_ffn_agg_b, L0_ffn_pn_gamma, L0_ffn_pn_beta, L0_ffn_d1_w, L0_ffn_d1_b, L0_ffn_d2_w, L0_ffn_d2_b, L0_ffn_bc_w, L0_ffn_bc_b, L0_ffn_gate_w, L0_ffn_gate_b, L0_ffn_out_gamma, L0_ffn_out_beta):
    import jax
    import jax.numpy as jnp

    def _L0_xattn_ref(hidden_q, kv_c, Wq, w_kc_q, w_kc_kv, W_qr, W_kr, Wo):
        import jax, jax.numpy as jnp
        import numpy as np
        B, S, L = (2, 128, 128)
        DIM_Q, H, K, D_C, D_CQ, R = (256, 16, 128, 64, 192, 64)

        def _rope_tables(seq_len, dim, dtype):
            inv_freq = 1.0 / 10000.0 ** (jnp.arange(0, dim, 2, dtype=dtype) / dim)
            t = jnp.arange(seq_len, dtype=dtype)
            freqs = t[:, None] * inv_freq[None, :]
            sin = jnp.repeat(jnp.sin(freqs), 2, axis=-1)
            cos = jnp.repeat(jnp.cos(freqs), 2, axis=-1)
            return (sin, cos)

        def _rotate_half(x):
            h = x.shape[-1] // 2
            return jnp.concatenate([-x[..., h:], x[..., :h]], axis=-1)
        b, s, _ = hidden_q.shape
        l = kv_c.shape[1]
        q_hk = (hidden_q @ Wq.T).reshape(b, s, H, K)
        q_big = jnp.einsum('bshk,hkq->bshq', q_hk, w_kc_q)
        sin, cos = _rope_tables(l, D_C, kv_c.dtype)
        kv_rope = kv_c * cos[None] + _rotate_half(kv_c) * sin[None]
        q_r = jnp.einsum('bshq,hqr->bhsr', q_big, W_qr)
        k_r = jnp.einsum('bld,hdr->bhlr', kv_rope, W_kr)
        scores = jnp.einsum('bhsr,bhlr->bhsl', q_r, k_r)
        attn = jax.nn.softmax(scores, axis=-1)
        ctx_c = jnp.einsum('bhsl,bld->bhsd', attn, kv_rope)
        ctx_lat = jnp.einsum('bhsd,hkd->bshk', ctx_c, w_kc_kv)
        out = ctx_lat.reshape(b, s, H * K) @ Wo.T
        return out

    def _L0_ffn_ref(x, in_gamma, in_beta, agg_w, agg_b, pn_gamma, pn_beta, d1_w, d1_b, d2_w, d2_b, bc_w, bc_b, gate_w, gate_b, out_gamma, out_beta):
        import jax, jax.numpy as jnp
        import numpy as np
        EPS = 1e-06
        K_STEPS = 4
        USE_GATING = True

        def layer_norm(x, gamma, beta):
            mu = jnp.mean(x, axis=-1, keepdims=True)
            var = jnp.mean(jnp.square(x - mu), axis=-1, keepdims=True)
            return (x - mu) * jax.lax.rsqrt(var + EPS) * gamma + beta
        x_norm = layer_norm(x, in_gamma, in_beta)
        thought = x_norm[:, -1, :] @ agg_w + agg_b
        for _ in range(K_STEPS):
            t = layer_norm(thought, pn_gamma, pn_beta)
            t = jax.nn.gelu(t @ d1_w + d1_b, approximate=False)
            thought = thought + (t @ d2_w + d2_b)
        broadcast = (thought @ bc_w + bc_b)[:, None, :]
        if USE_GATING:
            gate = jax.nn.sigmoid(x @ gate_w + gate_b)
            out = x + gate * broadcast
        else:
            out = x + broadcast
        return layer_norm(out, out_gamma, out_beta)
    x = x + jnp.tanh(g_xattn[0]) * _L0_xattn_ref(_layernorm(x, axis=-1), ctx_512, L0_xattn_Wq, L0_xattn_w_kc_q, L0_xattn_w_kc_kv, L0_xattn_W_qr, L0_xattn_W_kr, L0_xattn_Wo)
    x = x + jnp.tanh(g_ffn[0]) * _L0_ffn_ref(_layernorm(x, axis=-1), L0_ffn_in_gamma, L0_ffn_in_beta, L0_ffn_agg_w, L0_ffn_agg_b, L0_ffn_pn_gamma, L0_ffn_pn_beta, L0_ffn_d1_w, L0_ffn_d1_b, L0_ffn_d2_w, L0_ffn_d2_b, L0_ffn_bc_w, L0_ffn_bc_b, L0_ffn_gate_w, L0_ffn_gate_b, L0_ffn_out_gamma, L0_ffn_out_beta)
    return x

_drawn_inputs = setup_inputs


def setup_inputs(seed=0):
    import zlib

    import numpy as np

    out = dict(_drawn_inputs(seed))
    spreads = {'L0_ffn_in_gamma': (1.0, 0.2),
     'L0_ffn_in_beta': (0.0, 0.516),
     'L0_ffn_agg_b': (0.0, 0.1),
     'L0_ffn_pn_gamma': (1.0, 0.2),
     'L0_ffn_pn_beta': (0.0, 0.469),
     'L0_ffn_d1_b': (0.0, 0.1),
     'L0_ffn_d2_b': (0.0, 0.1),
     'L0_ffn_bc_b': (0.0, 0.1),
     'L0_ffn_gate_b': (0.0, 0.658),
     'L0_ffn_out_gamma': (1.0, 0.2),
     'L0_ffn_out_beta': (0.0, 0.1)}
    factors = {}
    for name, (base, spread) in spreads.items():
        noise = np.random.default_rng([zlib.crc32(name.encode()), seed]).standard_normal(out[name].shape)
        drawn = base * np.exp(spread * noise) if base else spread * noise
        out[name] = jnp.asarray(drawn.astype(out[name].dtype))
    for name, factor in factors.items():
        out[name] = (out[name] * factor).astype(out[name].dtype)
    return out
```

```python
from contextlib import ExitStack

import concourse.bass as bass
from concourse import mybir

F32 = mybir.dt.float32
F32R = mybir.dt.float32r
ALU = mybir.AluOpType
ACT = mybir.ActivationFunctionType
AX = mybir.AxisListType

P = 128
NB, S, D = 4, 256, 256
H, K, DC, DCQ, R = 16, 128, 64, 192, 64
HID = 1024
STEPS = 4
NU = NB * S // P
KB = D // P
LB = S // P
HG = 4
NG = H // HG
JQ = DCQ // 2
HB = HID // P
EPS_BLOCK, EPS_FFN = 1e-5, 1e-6
PROBS_BUFS = 3
OUT_BUFS = 3


def batch_of(u):
    return u % NB


def row_block_of(u):
    return 1 - u // NB


def thought_pieces():
    pieces = [[("c_stats", 0)], [("c_norm", 0), ("thoughtT", 0)], [("agg", 0), ("c_stats", 1)]]
    for k in range(STEPS):
        pieces += [[("c_norm", k + 1), ("thoughtT", k + 1)], [("up", k)]]
        pieces += [[("down", k)] + ([("c_stats", k + 2)] if k + 1 < STEPS else [])]
    return pieces + [[("thoughtT", STEPS + 1)], [("bc", 0)], [("bc_rows", 0), ("bc_rows", 1)]]


def make_plan():
    plan = [("kvT", 0), ("kvT", 1), ("x_stats", 0), ("x_stats", 1), ("x_norm", 0), ("x_norm", 1), ("xT", 0),
            ("wkrT", 0), ("wkrT", 1)]
    for g in range(NG + 3):
        if g < NG:
            plan += [("wkcqT", g, 0), ("wkcqT", g, 1)]
        if 1 <= g <= NG:
            plan += [("qrT", g - 1)]
        if 2 <= g <= NG + 1:
            plan += [("qk", g - 2)]
        if g >= 3:
            plan += [("foldA", g - 3), ("gq", 0, g - 3)]
        if g == 1:
            plan += [("x_stats", 2), ("x_stats", 3)]
        if g == 2:
            plan += [("x_norm", 2), ("x_norm", 3)]
    plan += [("vecT", 0)]
    pieces = thought_pieces()
    finals = []
    gated = []

    def some_thought(s, n):
        if s > NB + 1 or (s == NB + 1 and n >= 9):
            for _ in range(1):
                if pieces:
                    plan.extend(pieces.pop(0))

    def some_final():
        if not pieces and gated:
            u = gated.pop(0)
            plan.append(("f_pre", u))
            finals.append(u)
            if len(finals) > 1:
                plan.append(("f_norm", finals.pop(0)))

    for s in range(NU + 2):
        u = s - 1
        U = (s + 1) // 2
        new_pair = s % 2 == 1 and U < NU // 2
        for g in range(NG):
            if 0 <= u < NU:
                plan += [("st", u, g, lb) for lb in range(LB)]
            some_thought(s, 3 * g)
            if g == 0 and 0 <= u - 1 < NU:
                plan += [("ctxT", u - 1, 1)]
            if s < NU:
                plan += [("smax", s, j) for j in ([0, 1, 2], [3, 4, 5], [6, 7], [])[g]]
            if s == 0:
                plan += [("woT", 2 * g), ("woT", 2 * g + 1)] + ([("foldB", g - 1)] if g else [])
            if g and 0 <= u < NU:
                plan += [("pv", u, g - 1)]
            some_thought(s, 3 * g + 1)
            if g == 0 and new_pair:
                plan += [("xT", U)]
            if g == 0 and 0 <= u - 1 < NU and s == NU + 1:
                plan += [("out", u - 1)]
            if g == 1 and 0 <= u - 1 < NU and s <= NU:
                plan += [("out", u - 1)]
            if g == 2 and 0 <= u - 1 < NU:
                plan += [("y_norm", u - 1)]
            if g == 2 and s % 2 == 0 and s // 2 + 1 < NU // 2 and s:
                plan += [("x_stats", s + 2), ("x_stats", s + 3)]
            if g == 3:
                if s < NU:
                    plan += [("shiftT", s)]
                if 0 <= u < NU:
                    plan += [("ctxT", u, 0)]
                if 0 <= u - 1 < NU:
                    plan += [("yT", u - 1)]
                if s % 2 == 0 and s // 2 + 1 < NU // 2 and s:
                    plan += [("x_norm", s + 2), ("x_norm", s + 3)]
            some_thought(s, 3 * g + 2)
            some_final()
            if new_pair:
                plan += [("gq", U, g)]
        if s == 0:
            plan += [("foldB", NG - 1)]
        if 0 <= u < NU:
            plan += [("pv", u, NG - 1)]
        if 0 <= u - 1 < NU:
            plan += [("gate", u - 1)]
            gated.append(u - 1)
        some_final()
    while gated:
        some_final()
    plan += [("f_norm", u) for u in finals]
    return plan


RINGS = {
    "max_ring": ("wkrT", "qk", "smax"),
    "score_ring": ("wkcqT", "woT", "st"),
    "ctx_ring": ("qrT", "foldB", "pv"),
    "misc_ring": ("kvT", "xT", "vecT", "foldA", "gq", "shiftT", "ctxT", "out", "yT", "gate", "thoughtT", "agg",
                  "up", "down", "bc", "bc_rows"),
}
SPLIT = ("kvT", "xT", "foldA", "foldB", "gq", "ctxT")
STATS = ("x_stats", "y_stats", "c_stats", "f_pre")


def gated_cross_attention_ffn(nc, t, out):
    plan = []
    for entry in make_plan():
        plan.append(entry)
        if entry[0] == "out":
            plan.append(("y_stats", entry[1]))
    place, turn = {}, {}
    for r, (ring, stages) in enumerate(RINGS.items()):
        for n, entry in enumerate(e for e in plan if e[0] in stages):
            place[entry], turn[entry] = 2 * r + n % 2, n // 2

    def nth(stages):
        return {e: n + 1 for n, e in enumerate(e for e in plan if e[0] in stages)}

    split_n = nth(SPLIT)
    stats_n = nth(STATS)
    x_norm_n, y_norm_n, c_norm_n = nth(("x_norm",)), nth(("y_norm",)), nth(("c_norm",))
    f_norm_n = nth(("f_norm",))
    job = {e: n - 1 for e, n in stats_n.items()}
    jobs = len(job)

    with ExitStack() as ctx:
        def sb(name, shape, dt=F32, stack=ctx):
            return stack.enter_context(nc.sbuf_tensor(name, shape, dt))

        def sem(name):
            return ctx.enter_context(nc.semaphore(name))

        ps = ctx.enter_context(nc.psum_tensor("ps", [P, 8, 512], F32))

        consts = sb("consts", [P, P + 2 * LB * DC])
        ident = consts[:, 0:P]
        rope_cos = consts[:, P:P + LB * DC].rearrange("p (l d) -> p l d", l=LB)
        rope_sin = consts[:, P + LB * DC:P + 2 * LB * DC].rearrange("p (l d) -> p l d", l=LB)
        kv1 = sb("kv1", [P, NB, LB, DC + 1])
        kv_hi2 = sb("kv_hi2", [P, NB, S], F32R)
        kv_lo = sb("kv_lo", [P, NB, S], F32R)
        x = sb("x", [P, NU, D])
        normed = sb("normed", [P, NU, D])
        xT_hi = sb("xT_hi", [P, KB, 2 * P], F32R)
        xT_lo = sb("xT_lo", [P, KB, 2 * P], F32R)
        A_hi = sb("A_hi", [P, KB, H * DC], F32R)
        A_lo = sb("A_lo", [P, KB, H * DC], F32R)
        B_hi = sb("B_hi", [P, H // 2, D], F32R)
        B_lo = sb("B_lo", [P, H // 2, D], F32R)
        agg_w = sb("agg_w", [P, KB, D])
        bc_w = sb("bc_w", [P, KB, D])
        gate_w = sb("gate_w", [P, KB, D])
        vec_rows = sb("vec_rows", [16, P])
        vecs = sb("vecs", [P, 16])
        agg_b = sb("agg_b", [NB, D])
        d2_b = sb("d2_b", [NB, D])
        bc_b = sb("bc_b", [NB, D])
        gate_b = sb("gate_b", [P, D])
        out_gamma = sb("out_gamma", [P, D])
        out_beta = sb("out_beta", [P, D])
        g_raw = sb("g_raw", [P, 2])
        g_tanh = sb("g_tanh", [P, 2])
        bn6 = sb("bn6", [P, 2, 6])
        mean_var = sb("mean_var", [P, jobs, 2])
        var_eps = sb("var_eps", [P, jobs])
        rstd = sb("rstd", [P, jobs])
        minus_half = sb("minus_half", [P, 1])
        row_max = sb("row_max", [P, 2, H])
        shift = sb("shift", [H, 2, P], F32R)
        prob_sum_inv = sb("prob_sum_inv", [P, HG])
        yT = sb("yT", [P, KB, P])
        last_rows = sb("last_rows", [NB, D])
        thought = sb("thought", [NB, D])
        thought_bias = sb("thought_bias", [NB, D])
        thought_norm = sb("thought_norm", [NB, D])
        thoughtT = sb("thoughtT", [P, KB, NB])
        hid_in = sb("hid_in", [P, HB, NB])
        hid = sb("hid", [P, HB, NB])
        bc4 = sb("bc4", [NB, D])
        q_split = [sb("q_split0", [P, H, 2 * P], F32R)]
        q_hi = [sb("q_hi0", [P, H, 2 * P], F32R)]

        stage = ExitStack()
        ctxt = sb("ctxt", [P, NB, LB, DC], F32, stage)
        rope_t = sb("rope_t", [P, LB, DC], F32, stage)
        kv2 = sb("kv2", [P, NB, LB, 2, DC], F32, stage)
        wkr = sb("wkr", [P, H // 2, R], F32, stage)
        wkrT = sb("wkrT", [R, H * DC], F32, stage)
        wqr = sb("wqr", [JQ, H, 2, R], F32, stage)
        wkcq = sb("wkcq", [P, H, DCQ], F32, stage)
        wq = sb("wq", [P, H, D], F32, stage)
        wo = sb("wo", [P, KB, H * K], F32, stage)
        wkckv = sb("wkckv", [P, H, DC], F32, stage)
        wkcqT = sb("wkcqT", [JQ, 2, HG, 2, P], F32, stage)
        qrT = sb("qrT", [R, 2, HG * P], F32, stage)
        qk = sb("qk", [P, 2, HG * DC], F32, stage)
        woT = sb("woT", [P, 4, 2, D], F32, stage)
        stage.close()
        q_split.append(sb("q_split1", [P, H, 2 * P], F32R))
        q_hi.append(sb("q_hi1", [P, H, 2 * P], F32R))
        probs = sb("probs", [P, PROBS_BUFS, LB, HG * P])
        ctxn = sb("ctxn", [P, H * DC])
        ctxT_hi = sb("ctxT_hi", [P, H // 2, P], F32R)
        ctxT_lo = sb("ctxT_lo", [P, H // 2, P], F32R)
        gt = sb("gt", [P, NU, D])
        d2_w = sb("d2_w", [P, HB, D])
        bc_all = sb("bc_all", [P, NB, D])
        fin = sb("fin", [P, OUT_BUFS, D])
        row_pick = sb("row_pick", [NB, NB, P])
        d1_w = sb("d1_w", [P, KB, HID])

        full = [sem(f"full{i}") for i in range(8)]
        free = [sem(f"free{i}") for i in range(8)]
        hi_done = sem("hi_done")
        consts_in, ctx_in, row_pick_in = sem("consts_in"), sem("ctx_in"), sem("row_pick_in")
        x_in = [sem(f"x_in{i}") for i in range(3)]
        wkr_in = sem("wkr_in")
        wqr_in = [sem(f"wqr_in{g}") for g in range(NG)]
        wkcq_in = [sem(f"wkcq_in{g}") for g in range(NG)]
        wq_in = [sem(f"wq_in{g}") for g in range(NG)]
        wo_in = [sem(f"wo_in{i}") for i in range(2)]
        wkckv_in = sem("wkckv_in")
        vec_in, g_in, small_in = sem("vec_in"), sem("g_in"), sem("small_in")
        gate_w_in, agg_w_in, bc_w_in = sem("gate_w_in"), sem("agg_w_in"), sem("bc_w_in")
        d1_in, d2_in = sem("d1_in"), sem("d2_in")
        q_hi_in = [sem(f"q_hi_in{i}") for i in range(2)]
        shift_in = [sem(f"shift_in{i}") for i in range(2)]
        last_in = sem("last_in")
        stored = [sem(f"stored{i}") for i in range(OUT_BUFS)]
        kv_made = sem("kv_made")
        ones_row = sem("ones_row")
        g_tanh_made = sem("g_tanh_made")
        out_scaled = sem("out_scaled")
        stats_made = sem("stats_made")
        rstd_made = sem("rstd_made")
        x_normed, y_normed, c_normed = sem("x_normed"), sem("y_normed"), sem("c_normed")
        x2_biased = sem("x2_biased")
        gated = sem("gated")
        gelu_made = sem("gelu_made")
        fin_normed = sem("fin_normed")
        fin_made = sem("fin_made")
        dve_chain, pool_chain = sem("dve_chain"), sem("pool_chain")

        def bank(e):
            return ps[:, place[e], :]

        def claim(pe, e):
            if turn[e]:
                pe.wait_ge(free[place[e]], turn[e])

        def filled(eng, e):
            eng.wait_ge(full[place[e]], turn[e] + 1)

        def taken(eng, e):
            eng.wait_ge(free[place[e]], turn[e] + 1)

        block = ctx.enter_context(nc.Block())

        @block.sync
        def _(sp):
            x_rows = t["x"].rearrange("b (q p) d -> q p b d", p=P)
            sp.dma_start(consts[:, :], t["consts"]).then_inc(consts_in, 16)
            sp.dma_start(ctxt[:, :, :, :], t["ctx_512"].rearrange("b (l p) d -> p b l d", p=P)).then_inc(ctx_in, 16)
            sp.dma_start(x[:, 0:2, :], x_rows[1][:, 0:2, :]).then_inc(x_in[0], 16)
            sp.dma_start(wkr[:, :, :], t["L0_xattn_W_kr"].rearrange("(g two) d r -> (two d) g r", two=2)
                         ).then_inc(wkr_in, 16)
            for g in range(NG):
                hs = slice(HG * g, HG * (g + 1))
                sp.dma_start(wkcq[:, hs, :], t["L0_xattn_w_kc_q"].rearrange("h k q -> k h q")[:, hs, :]
                             ).then_inc(wkcq_in[g], 16)
                sp.dma_start(wqr[:, hs, :, :].rearrange("p h j r -> p h (j r)"),
                             t["L0_xattn_W_qr"].rearrange("h (p j) r -> p h (j r)", j=2)[:, hs, :]
                             ).then_inc(wqr_in[g], 16)
                sp.dma_start(wq[:, hs, :], t["L0_xattn_Wq"].rearrange("(h k) m -> k h m", k=K)[:, hs, :]
                             ).then_inc(wq_in[g], 16)
                if g == 0:
                    sp.dma_start(x[:, 2:4, :], x_rows[1][:, 2:4, :]).then_inc(x_in[1], 16)
                if g == 1:
                    sp.dma_start(g_raw[:, 0:1], t["g_xattn"].partition_broadcast(P)).then_inc(g_in, 16)
                    sp.dma_start(g_raw[:, 1:2], t["g_ffn"].partition_broadcast(P)).then_inc(g_in, 16)
            for i in range(2):
                cols = slice(i * H * K // 2, (i + 1) * H * K // 2)
                sp.dma_start(wo[:, :, cols], t["L0_xattn_Wo"].rearrange("(b p) n -> p b n", p=P)[:, :, cols]
                             ).then_inc(wo_in[i], 16)
                if i == 0:
                    sp.dma_start(wkckv[:, :, :], t["L0_xattn_w_kc_kv"].rearrange("h k d -> k h d")
                                 ).then_inc(wkckv_in, 16)
            sp.dma_start(x[:, NB:NU, :], x_rows[0]).then_inc(x_in[2], 16)
            for i, name in enumerate(("in_gamma", "in_beta", "pn_gamma", "pn_beta")):
                sp.dma_start(vec_rows[2 * i:2 * i + 2, :], t["L0_ffn_" + name].rearrange("(b p) -> b p", p=P)
                             ).then_inc(vec_in, 16)
            sp.dma_start(vec_rows[8:16, :], t["L0_ffn_d1_b"].rearrange("(b p) -> b p", p=P)).then_inc(vec_in, 16)
            sp.dma_start(gate_w[:, :, :], t["L0_ffn_gate_w"].rearrange("(b p) n -> p b n", p=P)
                         ).then_inc(gate_w_in, 16)
            sp.dma_start(gate_b[:, :], t["L0_ffn_gate_b"].partition_broadcast(P)).then_inc(small_in, 16)
            sp.dma_start(out_gamma[:, :], t["L0_ffn_out_gamma"].partition_broadcast(P)).then_inc(small_in, 16)
            sp.dma_start(out_beta[:, :], t["L0_ffn_out_beta"].partition_broadcast(P)).then_inc(small_in, 16)
            sp.dma_start(agg_b[:, :], t["L0_ffn_agg_b"].partition_broadcast(NB)).then_inc(small_in, 16)
            sp.dma_start(d2_b[:, :], t["L0_ffn_d2_b"].partition_broadcast(NB)).then_inc(small_in, 16)
            sp.dma_start(bc_b[:, :], t["L0_ffn_bc_b"].partition_broadcast(NB)).then_inc(small_in, 16)
            sp.dma_start(agg_w[:, :, :], t["L0_ffn_agg_w"].rearrange("(b p) n -> p b n", p=P)).then_inc(agg_w_in, 16)
            sp.dma_start(bc_w[:, :, :], t["L0_ffn_bc_w"].rearrange("(b p) n -> p b n", p=P)).then_inc(bc_w_in, 16)
            out_rows = out.rearrange("b (q p) d -> q p b d", p=P)
            for e in plan:
                if e == ("st", 0, 1, 0):
                    filled(sp, ("foldA", NG - 1))
                    filled(sp, ("foldB", NG - 1))
                    sp.dma_start(d1_w[:, :, :], t["L0_ffn_d1_w"].rearrange("(b p) n -> p b n", p=P)
                                 ).then_inc(d1_in, 16)
                    sp.dma_start(d2_w[:, :, :], t["L0_ffn_d2_w"].rearrange("(b p) n -> p b n", p=P)
                                 ).then_inc(d2_in, 16)
                    sp.dma_start(row_pick[:, :, :], t["row_pick"]).then_inc(row_pick_in, 16)
                if e[0] == "gq" and e[2] == NG - 1:
                    U = e[1]
                    sp.wait_ge(hi_done, split_n[e])
                    for odd in range(2):
                        src = q_split[U % 2][64 * odd:64 * odd + 64, :, :].rearrange("p (g two) q -> p g two q", two=2)
                        dst = q_hi[U % 2][0:64, :, :].rearrange("p (g two) q -> p g two q", two=2)
                        sp.dma_start(dst[:, :, odd, :].bitcast(F32), src[:, :, odd, :].bitcast(F32)).then_inc(q_hi_in[U % 2], 16)
                if e[0] == "shiftT":
                    s = e[1]
                    taken(sp, e)
                    sp.dma_start(q_hi[s // 2 % 2][64:65, :, s % 2 * P:s % 2 * P + P].bitcast(F32),
                                 shift[:, s % 2, :].bitcast(F32)
                                 ).then_inc(shift_in[s % 2], 16)
                if e[0] == "y_norm" and e[1] < NB:
                    sp.wait_ge(y_normed, y_norm_n[e])
                    sp.dma_start(last_rows[e[1]:e[1] + 1, :], normed[P - 1:P, e[1], :]).then_inc(last_in, 16)
                if e[0] == "f_norm":
                    u, n = e[1], f_norm_n[e]
                    sp.wait_ge(fin_made, n)
                    sp.dma_start(out_rows[row_block_of(u)][:, batch_of(u), :], fin[:, (n - 1) % OUT_BUFS, :]
                                 ).then_inc(stored[(n - 1) % OUT_BUFS], 16)
            for i in range(OUT_BUFS):
                sp.wait_ge(stored[i], 16 * len(range(i, NU, OUT_BUFS)))

        @block.gpsimd
        def _(pool):
            chained = [0]

            def link(ins):
                chained[0] += 1
                ins.then_inc(pool_chain, 1)
                pool.wait_ge(pool_chain, chained[0])

            pool.memset(minus_half[:, :], -0.5)
            link(pool.memset(kv1[:, :, :, DC:DC + 1], 1.0))
            pool.wait_ge(consts_in, 16)
            pool.wait_ge(ctx_in, 16)
            half = DC // 2
            for b in range(NB):
                kv = kv1[:, b, :, 0:DC]
                pool.tensor_tensor(kv, ctxt[:, b], rope_cos, ALU.mult)
                pool.tensor_tensor(rope_t[:, :, 0:half], ctxt[:, b, :, half:DC], rope_sin[:, :, 0:half], ALU.mult)
                link(pool.tensor_tensor(rope_t[:, :, half:DC], ctxt[:, b, :, 0:half], rope_sin[:, :, half:DC],
                                        ALU.mult))
                link(pool.tensor_tensor(kv, kv, rope_t[:, :, :], ALU.add))
                pool.tensor_copy(kv2[:, b, :, 0, :], kv)
                pool.tensor_copy(kv2[:, b, :, 1, :], kv).then_inc(kv_made, 1)

            for e in plan:
                if e[0] in STATS:
                    n = job[e]
                    rows = NB if e[0] == "c_stats" else P
                    eps = EPS_FFN if e[0] in ("c_stats", "f_pre") else EPS_BLOCK
                    pool.wait_ge(stats_made, stats_n[e])
                    link(pool.tensor_scalar(var_eps[0:rows, n:n + 1], mean_var[0:rows, n, 1:2], eps, None, ALU.add))
                    pool.tensor_tensor(rstd[0:rows, n:n + 1], var_eps[0:rows, n:n + 1], minus_half[0:rows, :],
                                       ALU.pow).then_inc(rstd_made, 1)
                if e == ("smax", 0, 0):
                    pool.wait_ge(g_tanh_made, 1)
                    pool.wait_ge(small_in, 16 * 6)
                    pool.tensor_scalar(out_gamma[:, :], out_gamma[:, :], g_tanh[:, 1:2], None, ALU.mult)
                    link(pool.tensor_scalar(out_beta[:, :], out_beta[:, :], g_tanh[:, 1:2], None, ALU.mult))
                if e[0] == "y_norm":
                    u = e[1]
                    pool.wait_ge(y_normed, y_norm_n[e])
                    pool.tensor_tensor(x[:, u, :], x[:, u, :], out_beta[:, :], ALU.add).then_inc(x2_biased, 1)
                if e[0] == "f_norm":
                    u, n = e[1], f_norm_n[e]
                    f = fin[:, (n - 1) % OUT_BUFS, :]
                    pool.wait_ge(fin_normed, n)
                    pool.wait_ge(x2_biased, u + 1)
                    link(pool.tensor_tensor(f, f, out_gamma[:, :], ALU.mult))
                    pool.tensor_tensor(f, f, x[:, u, :], ALU.add).then_inc(fin_made, 1)

        @block.scalar
        def _(act):
            act.wait_ge(g_in, 32)
            act.activation(g_tanh[:, :], g_raw[:, :], ACT.Tanh).then_inc(g_tanh_made, 1)
            for e in plan:
                name = e[0]
                if name == "kvT":
                    filled(act, e)
                    act.activation(kv_hi2[:, 2 * e[1]:2 * e[1] + 2, :].rearrange("p b l -> p (b l)"), bank(e),
                                   ACT.Copy).then_inc(hi_done, 1)
                if name == "xT":
                    filled(act, e)
                    act.activation(xT_hi[:, :, :].rearrange("p k q -> p (k q)"), bank(e), ACT.Copy
                                   ).then_inc(hi_done, 1)
                if name == "wkrT":
                    filled(act, e)
                    act.activation(wkrT[:, 512 * e[1]:512 * e[1] + 512], bank(e)[0:R, :], ACT.Copy
                                   ).then_inc(free[place[e]], 1)
                if name == "wkcqT" and e[2] == 0:
                    filled(act, e)
                    act.activation(wkcqT[:, e[1] % 2, 0:2].rearrange("p h j k -> p (h j k)"), bank(e)[0:JQ, :],
                                   ACT.Copy).then_inc(free[place[e]], 1)
                if name == "qk":
                    filled(act, e)
                    act.activation(qk[:, e[1] % 2, :], bank(e)[:, 0:HG * DC], ACT.Copy).then_inc(free[place[e]], 1)
                if name == "foldA":
                    filled(act, e)
                    cols = slice(HG * DC * e[1], HG * DC * (e[1] + 1))
                    act.activation(A_hi[:, :, cols], bank(e).rearrange("p (k n) -> p k n", k=KB), ACT.Copy
                                   ).then_inc(hi_done, 1)
                if name == "woT" and e[1] % 2 == 0:
                    filled(act, e)
                    act.activation(woT[:, e[1] % 4].rearrange("p h m -> p (h m)"), bank(e), ACT.Copy
                                   ).then_inc(free[place[e]], 1)
                if name == "foldB":
                    filled(act, e)
                    act.activation(B_hi[:, 2 * e[1]:2 * e[1] + 2, :].rearrange("p g m -> p (g m)"), bank(e), ACT.Copy
                                   ).then_inc(hi_done, 1)
                if name == "gq":
                    _, U, j = e
                    dst = q_split[U % 2][:, HG * j:HG * j + HG, :].rearrange("p (g two) q -> p g two q", two=2)
                    src = bank(e).rearrange("p (g q) -> p g q", g=2)
                    filled(act, e)
                    act.activation(dst[0:64, :, 0, :], src[0:64], ACT.Copy)
                    act.activation(dst[64:128, :, 1, :], src[64:128], ACT.Copy).then_inc(hi_done, 1)
                if name == "shiftT":
                    filled(act, e)
                    act.activation(shift[:, e[1] % 2, :], bank(e)[0:H, 0:P], ACT.Copy, scale=-1.0
                                   ).then_inc(free[place[e]], 1)
                if name == "st":
                    _, u, g, lb = e
                    n = u * NG + g
                    if n >= PROBS_BUFS:
                        m = n - PROBS_BUFS
                        filled(act, ("pv", m // NG, m % NG))
                    filled(act, e)
                    act.activation(probs[:, n % PROBS_BUFS, lb, :], bank(e), ACT.Exp).then_inc(free[place[e]], 1)
                if name == "ctxT":
                    filled(act, e)
                    act.activation(ctxT_hi[:, 4 * e[2]:4 * e[2] + 4, :].rearrange("p g q -> p (g q)"), bank(e),
                                   ACT.Copy).then_inc(hi_done, 1)
                if name == "yT":
                    filled(act, e)
                    act.activation(yT[:, :, :].rearrange("p k q -> p (k q)"), bank(e)[:, 0:KB * P], ACT.Copy
                                   ).then_inc(free[place[e]], 1)
                if name == "gate":
                    u = e[1]
                    taken(act, e)
                    act.activation(gt[:, u, :], gt[:, u, :], ACT.Tanh, scale=0.5).then_inc(gated, 1)
                if name == "up":
                    taken(act, e)
                    act.activation(hid[:, :, :], hid_in[:, :, :], ACT.Gelu).then_inc(gelu_made, 1)
                if name == "bc_rows":
                    filled(act, e)
                    act.activation(bc_all[:, 2 * e[1]:2 * e[1] + 2, :].rearrange("p b d -> p (b d)"), bank(e),
                                   ACT.Copy).then_inc(free[place[e]], 1)

        @block.vector
        def _(dve):
            chained = [0]

            def link(ins):
                chained[0] += 1
                ins.then_inc(dve_chain, 1)
                dve.wait_ge(dve_chain, chained[0])

            def stats(rows, src, e):
                if stats_n[e] > 1:
                    dve.wait_ge(stats_made, stats_n[e] - 1)
                link(dve.bn_stats(bn6[0:rows, 0, :], src))
                dve.bn_aggr(mean_var[0:rows, job[e], :], bn6[0:rows, 0, :]).then_inc(stats_made, 1)

            def normalise(rows, dst, src, e):
                n = job[e]
                dve.wait_ge(rstd_made, stats_n[e])
                return dve.tensor_scalar(dst, src, mean_var[0:rows, n, 0:1], rstd[0:rows, n:n + 1], ALU.subtract,
                                         ALU.mult)

            dve.memset(kv_lo[64:65, :, :].bitcast(F32), 1.0).then_inc(ones_row, 1)
            for e in plan:
                name = e[0]
                if name == "x_stats":
                    u = e[1]
                    if u % NB % 2 == 0:
                        dve.wait_ge(x_in[min(u // 2, 2)], 16)
                    stats(P, x[:, u, :], e)
                if name == "x_norm":
                    u = e[1]
                    normalise(P, normed[:, u, :], x[:, u, :], ("x_stats", u)).then_inc(x_normed, 1)
                if name == "kvT":
                    dve.wait_ge(hi_done, split_n[e])
                    bs = slice(2 * e[1], 2 * e[1] + 2)
                    dve.tensor_tensor(kv_lo[0:64, bs, :].rearrange("p b l -> p (b l)"), bank(e)[0:64, :],
                                      kv_hi2[0:64, bs, :].rearrange("p b l -> p (b l)").bitcast(F32), ALU.subtract
                                      ).then_inc(free[place[e]], 1)
                if name == "xT":
                    dve.wait_ge(hi_done, split_n[e])
                    dve.tensor_tensor(xT_lo[:, :, :].rearrange("p k q -> p (k q)"), bank(e),
                                      xT_hi[:, :, :].rearrange("p k q -> p (k q)").bitcast(F32), ALU.subtract
                                      ).then_inc(free[place[e]], 1)
                if name == "wkcqT" and e[2] == 1:
                    filled(dve, e)
                    dve.tensor_copy(wkcqT[:, e[1] % 2, 2:4].rearrange("p h j k -> p (h j k)"), bank(e)[0:JQ, :]
                                    ).then_inc(free[place[e]], 1)
                if name == "qrT":
                    filled(dve, e)
                    dve.tensor_copy(qrT[:, e[1] % 2, :], bank(e)[0:R, :]).then_inc(free[place[e]], 1)
                if name == "foldA":
                    dve.wait_ge(hi_done, split_n[e])
                    cols = slice(HG * DC * e[1], HG * DC * (e[1] + 1))
                    dve.tensor_tensor(A_lo[:, :, cols], bank(e).rearrange("p (k n) -> p k n", k=KB),
                                      A_hi[:, :, cols].bitcast(F32), ALU.subtract).then_inc(free[place[e]], 1)
                if name == "woT" and e[1] % 2 == 1:
                    filled(dve, e)
                    dve.tensor_copy(woT[:, e[1] % 4].rearrange("p h m -> p (h m)"), bank(e)
                                    ).then_inc(free[place[e]], 1)
                if name == "foldB":
                    dve.wait_ge(hi_done, split_n[e])
                    gs = slice(2 * e[1], 2 * e[1] + 2)
                    dve.tensor_tensor(B_lo[:, gs, :].rearrange("p g m -> p (g m)"), bank(e),
                                      B_hi[:, gs, :].rearrange("p g m -> p (g m)").bitcast(F32), ALU.subtract
                                      ).then_inc(free[place[e]], 1)
                if name == "vecT":
                    filled(dve, e)
                    dve.tensor_copy(vecs[:, :], bank(e)[:, 0:16]).then_inc(free[place[e]], 1)
                if name == "gq":
                    _, U, j = e
                    dst = q_split[U % 2][:, HG * j:HG * j + HG, :].rearrange("p (g two) q -> p g two q", two=2)
                    src = bank(e).rearrange("p (g q) -> p g q", g=2)
                    dve.wait_ge(hi_done, split_n[e])
                    dve.tensor_tensor(dst[64:128, :, 0, :], src[0:64], dst[0:64, :, 0, :].bitcast(F32), ALU.subtract)
                    dve.tensor_tensor(dst[0:64, :, 1, :], src[64:128], dst[64:128, :, 1, :].bitcast(F32), ALU.subtract
                                      ).then_inc(free[place[e]], 1)
                if name == "smax":
                    _, s, j = e
                    filled(dve, e)
                    dve.reduce_max(row_max[:, s % 2, 2 * j:2 * j + 2], bank(e).rearrange("p (h l) -> p h l", h=2), AX.X
                                   ).then_inc(free[place[e]], 1)
                if name == "pv":
                    _, u, g = e
                    if (u, g) != (0, 0):
                        taken(dve, ("pv", u, g - 1) if g else ("pv", u - 1, NG - 1))
                    filled(dve, e)
                    r = bank(e)[:, 0:HG * (DC + 1)].rearrange("p (h d) -> p h d", h=HG)
                    link(dve.reciprocal(prob_sum_inv[:, :].unsqueeze(2), r[:, :, DC:DC + 1]))
                    dve.tensor_tensor(ctxn[:, HG * DC * g:HG * DC * (g + 1)].rearrange("p (h d) -> p h d", h=HG),
                                      r[:, :, 0:DC], prob_sum_inv[:, :].unsqueeze(2).to_broadcast([P, HG, DC]),
                                      ALU.mult).then_inc(free[place[e]], 1)
                if name == "ctxT":
                    gs = slice(4 * e[2], 4 * e[2] + 4)
                    dve.wait_ge(hi_done, split_n[e])
                    dve.tensor_tensor(ctxT_lo[:, gs, :].rearrange("p g q -> p (g q)"), bank(e),
                                      ctxT_hi[:, gs, :].rearrange("p g q -> p (g q)").bitcast(F32), ALU.subtract
                                      ).then_inc(free[place[e]], 1)
                if name == "out":
                    u = e[1]
                    if u == 0:
                        dve.wait_ge(g_tanh_made, 1)
                    filled(dve, e)
                    ins = dve.scalar_tensor_tensor(x[:, u, :], bank(e)[:, 0:D], g_tanh[:, 0:1], x[:, u, :], ALU.mult,
                                                   ALU.add)
                    ins.then_inc(free[place[e]], 1)
                    taken(dve, e)
                if name == "y_stats":
                    stats(P, x[:, e[1], :], e)
                if name == "y_norm":
                    u = e[1]
                    normalise(P, normed[:, u, :], x[:, u, :], ("y_stats", u)).then_inc(y_normed, 1)
                if name == "gate":
                    if e[1] == 0:
                        dve.wait_ge(small_in, 16 * 6)
                    filled(dve, e)
                    dve.tensor_tensor(gt[:, e[1], :], bank(e)[:, 0:D], gate_b[:, :], ALU.add
                                      ).then_inc(free[place[e]], 1)
                if name == "c_stats":
                    if e[1] == 0:
                        dve.wait_ge(last_in, 16 * NB)
                    stats(NB, (last_rows if e[1] == 0 else thought)[:, :], e)
                if name == "c_norm":
                    k = e[1]
                    normalise(NB, thought_norm[:, :], (last_rows if k == 0 else thought)[:, :], ("c_stats", k)
                              ).then_inc(c_normed, 1)
                    if k:
                        link(dve.tensor_tensor(thought_bias[:, :], thought[:, :], d2_b[:, :], ALU.add))
                if name == "thoughtT":
                    k = e[1]
                    filled(dve, e)
                    cols = bank(e)[:, 0:KB * NB].rearrange("p (k b) -> p k b", k=KB)
                    if k == STEPS + 1:
                        dve.tensor_copy(thoughtT[:, :, :], cols).then_inc(free[place[e]], 1)
                    else:
                        c = 0 if k == 0 else 4
                        for kb in range(KB):
                            ins = dve.tensor_scalar(thoughtT[:, kb, :], cols[:, kb, :], vecs[:, c + kb:c + kb + 1],
                                                    vecs[:, c + KB + kb:c + KB + kb + 1], ALU.mult, ALU.add)
                        ins.then_inc(free[place[e]], 1)
                if name == "agg":
                    filled(dve, e)
                    dve.tensor_tensor(thought[:, :], bank(e)[0:NB, 0:D], agg_b[:, :], ALU.add
                                      ).then_inc(free[place[e]], 1)
                    taken(dve, e)
                if name == "up":
                    filled(dve, e)
                    dve.tensor_tensor(hid_in[:, :, :], bank(e)[:, 0:HB * NB].rearrange("p (j b) -> p j b", j=HB),
                                      vecs[:, 8:8 + HB].unsqueeze(2).to_broadcast([P, HB, NB]), ALU.add
                                      ).then_inc(free[place[e]], 1)
                if name == "down":
                    filled(dve, e)
                    dve.tensor_tensor(thought[:, :], bank(e)[0:NB, 0:D], thought_bias[:, :], ALU.add
                                      ).then_inc(free[place[e]], 1)
                    taken(dve, e)
                if name == "bc":
                    filled(dve, e)
                    link(dve.tensor_tensor(bc4[:, :], bank(e)[0:NB, 0:D], bc_b[:, :], ALU.add))
                    dve.tensor_scalar(bc4[:, :], bc4[:, :], 0.5, None, ALU.mult).then_inc(free[place[e]], 1)
                if name == "f_pre":
                    u = e[1]
                    dve.wait_ge(gated, u + 1)
                    if u == 0:
                        for i in range(2):
                            taken(dve, ("bc_rows", i))
                    link(dve.scalar_tensor_tensor(gt[:, u, :], gt[:, u, :], 1.0, bc_all[:, batch_of(u), :], ALU.add,
                                                  ALU.mult))
                    link(dve.tensor_tensor(gt[:, u, :], gt[:, u, :], normed[:, u, :], ALU.add))
                    stats(P, gt[:, u, :], e)
                if name == "f_norm":
                    u, n = e[1], f_norm_n[e]
                    if n > OUT_BUFS:
                        dve.wait_ge(stored[(n - 1) % OUT_BUFS], 16 * ((n - 1) // OUT_BUFS))
                    normalise(P, fin[:, (n - 1) % OUT_BUFS, :], gt[:, u, :], ("f_pre", u)).then_inc(fin_normed, 1)

        @block.tensor
        def _(pe):
            def split_product(dst, a_hi, a_lo, b_hi, b_lo, first, last):
                pe.matmul(dst, a_hi, b_lo, start=first, stop=False)
                pe.matmul(dst, a_hi, b_hi, start=False, stop=False)
                return pe.matmul(dst, a_lo, b_hi, start=False, stop=last)

            for e in plan:
                name = e[0]
                done = full[place[e]] if e in place else None
                if e in place:
                    claim(pe, e)
                if name == "kvT":
                    pe.wait_ge(kv_made, 2 * e[1] + 2)
                    for i in range(2 * LB):
                        b, lb = 2 * e[1] + i // LB, i % LB
                        ins = pe.transpose(bank(e)[:, i * P:(i + 1) * P],
                                           kv2[:, b, lb].rearrange("p two d -> p (two d)"), ident)
                    ins.then_inc(done, 1)
                if name == "xT":
                    U = e[1]
                    pe.wait_ge(x_normed, 2 * U + 2)
                    for kb in range(KB):
                        for i in range(2):
                            ins = pe.transpose(bank(e)[:, kb * 2 * P + i * P:kb * 2 * P + (i + 1) * P],
                                               normed[:, 2 * U + i, kb * P:(kb + 1) * P], ident)
                    ins.then_inc(done, 1)
                if name == "wkrT":
                    pe.wait_ge(wkr_in, 16)
                    for i in range(4):
                        ins = pe.transpose(bank(e)[0:R, i * P:(i + 1) * P], wkr[:, 4 * e[1] + i, :], ident)
                    ins.then_inc(done, 1)
                if name == "wkcqT":
                    _, g, i = e
                    pe.wait_ge(wkcq_in[g], 16)
                    for hh in range(2):
                        for j in range(2):
                            c = (2 * hh + j) * P
                            ins = pe.transpose(bank(e)[0:JQ, c:c + P], wkcq[:, HG * g + 2 * i + hh, j:DCQ:2], ident)
                    ins.then_inc(done, 1)
                if name == "qrT":
                    g = e[1]
                    pe.wait_ge(wqr_in[g], 16)
                    taken(pe, ("wkcqT", g, 0))
                    taken(pe, ("wkcqT", g, 1))
                    for hh in range(HG):
                        for j in range(2):
                            ins = pe.matmul(bank(e)[0:R, hh * P:(hh + 1) * P], wqr[:, HG * g + hh, j, :],
                                            wkcqT[:, g % 2, hh, j, :], start=(j == 0), stop=(j == 1))
                    ins.then_inc(done, 1)
                if name == "qk":
                    g = e[1]
                    taken(pe, ("qrT", g))
                    if g == 0:
                        taken(pe, ("wkrT", 0))
                        taken(pe, ("wkrT", 1))
                    for hh in range(HG):
                        h = HG * g + hh
                        ins = pe.matmul(bank(e)[:, hh * DC:(hh + 1) * DC], qrT[:, g % 2, hh * P:(hh + 1) * P],
                                        wkrT[:, h * DC:(h + 1) * DC], start=True, stop=True)
                    ins.then_inc(done, 1)
                if name == "foldA":
                    g = e[1]
                    pe.wait_ge(wq_in[g], 16)
                    taken(pe, ("qk", g))
                    for hh in range(HG):
                        for kb in range(KB):
                            c = kb * HG * DC + hh * DC
                            ins = pe.matmul(bank(e)[:, c:c + DC], wq[:, HG * g + hh, kb * P:(kb + 1) * P],
                                            qk[:, g % 2, hh * DC:(hh + 1) * DC], start=True, stop=True)
                    ins.then_inc(done, 1)
                if name == "woT":
                    i = e[1]
                    pe.wait_ge(wo_in[i // 4], 16)
                    for hh in range(2):
                        for kb in range(KB):
                            c = hh * D + kb * P
                            h = 2 * i + hh
                            ins = pe.transpose(bank(e)[:, c:c + P], wo[:, kb, h * K:(h + 1) * K], ident)
                    ins.then_inc(done, 1)
                if name == "foldB":
                    i = e[1]
                    pe.wait_ge(wkckv_in, 16)
                    taken(pe, ("woT", 2 * i))
                    taken(pe, ("woT", 2 * i + 1))
                    for hh in range(HG):
                        h = HG * i + hh
                        ins = pe.matmul(bank(e)[64 * (hh % 2):64 * (hh % 2) + 64, hh // 2 * D:(hh // 2 + 1) * D],
                                        wkckv[:, h, :], woT[:, h // 2 % 4, hh % 2, :], start=True, stop=True)
                    ins.then_inc(done, 1)
                if name == "vecT":
                    pe.wait_ge(vec_in, 16 * 5)
                    pe.transpose(bank(e)[:, 0:16], vec_rows[:, :], ident[0:16, 0:16]).then_inc(done, 1)
                if name == "gq":
                    _, U, j = e
                    taken(pe, ("foldA", j))
                    taken(pe, ("xT", U))
                    for i in range(2):
                        c = (2 * j + i) * P
                        for kb in range(KB):
                            ins = split_product(bank(e)[:, i * 2 * P:(i + 1) * 2 * P], A_hi[:, kb, c:c + P],
                                                A_lo[:, kb, c:c + P], xT_hi[:, kb, :], xT_lo[:, kb, :],
                                                kb == 0, kb == KB - 1)
                    ins.then_inc(done, 1)
                if name == "smax":
                    _, s, j = e
                    if j == 0 and s == 0:
                        taken(pe, ("kvT", 0))
                        taken(pe, ("kvT", 1))
                    if s % 2 == 0 and j % 2 == 0:
                        taken(pe, ("gq", s // 2, j // 2))
                    for i in range(2):
                        ins = pe.matmul(bank(e)[:, i * S:(i + 1) * S],
                                        q_split[s // 2 % 2][:, 2 * j + i, s % 2 * P:s % 2 * P + P],
                                        kv_hi2[:, batch_of(s), :], start=True, stop=True)
                    ins.then_inc(done, 1)
                if name == "shiftT":
                    s = e[1]
                    taken(pe, ("smax", s, 6))
                    taken(pe, ("smax", s, 7))
                    pe.transpose(bank(e)[0:H, 0:P], row_max[:, s % 2, :], ident).then_inc(done, 1)
                if name == "st":
                    _, u, g, lb = e
                    U = u // 2
                    q = slice(u % 2 * P, u % 2 * P + P)
                    hs = slice(HG * g, HG * (g + 1))
                    if g == 0 and lb == 0:
                        pe.wait_ge(q_hi_in[U % 2], 32 * (U // 2 + 1))
                        pe.wait_ge(shift_in[u % 2], 16 * (u // 2 + 1))
                        if u == 0:
                            pe.wait_ge(ones_row, 1)
                    dst = bank(e).rearrange("p (h q) -> p h q", h=HG)
                    pe.matmul(dst, kv_lo[0:65, batch_of(u), lb * P:(lb + 1) * P], q_hi[U % 2][0:65, hs, q],
                              start=True, stop=False)
                    pe.matmul(dst, kv_hi2[:, batch_of(u), lb * P:(lb + 1) * P], q_split[U % 2][:, hs, q],
                              start=False, stop=True).then_inc(done, 1)
                if name == "pv":
                    _, u, g = e
                    n = u * NG + g
                    taken(pe, ("st", u, g, LB - 1))
                    taken(pe, ("st", u, g, 0))
                    for hh in range(HG):
                        for lb in range(LB):
                            ins = pe.matmul(bank(e)[:, hh * (DC + 1):(hh + 1) * (DC + 1)],
                                            probs[:, n % PROBS_BUFS, lb, hh * P:(hh + 1) * P],
                                            kv1[:, batch_of(u), lb, :], start=(lb == 0), stop=(lb == LB - 1))
                    ins.then_inc(done, 1)
                if name == "ctxT":
                    _, u, half = e
                    taken(pe, ("pv", u, 2 * half))
                    taken(pe, ("pv", u, 2 * half + 1))
                    for i in range(4):
                        c = (4 * half + i) * P
                        ins = pe.transpose(bank(e)[:, i * P:(i + 1) * P], ctxn[:, c:c + P], ident)
                    ins.then_inc(done, 1)
                if name == "out":
                    u = e[1]
                    taken(pe, ("ctxT", u, 0))
                    taken(pe, ("ctxT", u, 1))
                    if u == 0:
                        for i in range(NG):
                            taken(pe, ("foldB", i))
                    for i in range(H // 2):
                        ins = split_product(bank(e)[:, 0:D], ctxT_hi[:, i, :], ctxT_lo[:, i, :], B_hi[:, i, :],
                                            B_lo[:, i, :], i == 0, i == H // 2 - 1)
                    ins.then_inc(done, 1)
                if name == "yT":
                    u = e[1]
                    pe.wait_ge(y_normed, y_norm_n[("y_norm", u)])
                    for kb in range(KB):
                        ins = pe.transpose(bank(e)[:, kb * P:(kb + 1) * P], normed[:, u, kb * P:(kb + 1) * P], ident)
                    ins.then_inc(done, 1)
                if name == "gate":
                    u = e[1]
                    pe.wait_ge(gate_w_in, 16)
                    taken(pe, ("yT", u))
                    for kb in range(KB):
                        ins = pe.matmul(bank(e)[:, 0:D], yT[:, kb, :], gate_w[:, kb, :], start=(kb == 0),
                                        stop=(kb == KB - 1))
                    ins.then_inc(done, 1)
                if name == "thoughtT":
                    k = e[1]
                    src = thought_norm if k <= STEPS else thought
                    if k <= STEPS:
                        pe.wait_ge(c_normed, c_norm_n[("c_norm", k)])
                    else:
                        taken(pe, ("down", STEPS - 1))
                    if k == 0:
                        taken(pe, ("vecT", 0))
                    for kb in range(KB):
                        ins = pe.transpose(bank(e)[:, kb * NB:(kb + 1) * NB], src[:, kb * P:(kb + 1) * P],
                                           ident[0:NB, 0:NB])
                    ins.then_inc(done, 1)
                if name in ("agg", "bc"):
                    taken(pe, ("thoughtT", 0 if name == "agg" else STEPS + 1))
                    w = agg_w if name == "agg" else bc_w
                    pe.wait_ge(agg_w_in if name == "agg" else bc_w_in, 16)
                    for kb in range(KB):
                        ins = pe.matmul(bank(e)[0:NB, 0:D], thoughtT[:, kb, :], w[:, kb, :], start=(kb == 0),
                                        stop=(kb == KB - 1))
                    ins.then_inc(done, 1)
                if name == "up":
                    taken(pe, ("thoughtT", e[1] + 1))
                    if e[1] == 0:
                        pe.wait_ge(d1_in, 16)
                    for j in range(HB):
                        for kb in range(KB):
                            ins = pe.matmul(bank(e)[:, j * NB:(j + 1) * NB], d1_w[:, kb, j * P:(j + 1) * P],
                                            thoughtT[:, kb, :], start=(kb == 0), stop=(kb == KB - 1))
                    ins.then_inc(done, 1)
                if name == "down":
                    pe.wait_ge(gelu_made, e[1] + 1)
                    if e[1] == 0:
                        pe.wait_ge(d2_in, 16)
                    for j in range(HB):
                        ins = pe.matmul(bank(e)[0:NB, 0:D], hid[:, j, :], d2_w[:, j, :], start=(j == 0),
                                        stop=(j == HB - 1))
                    ins.then_inc(done, 1)
                if name == "bc_rows":
                    taken(pe, ("bc", 0))
                    pe.wait_ge(row_pick_in, 16)
                    for i in range(2):
                        ins = pe.matmul(bank(e)[:, i * D:(i + 1) * D], row_pick[:, 2 * e[1] + i, :], bc4[:, :],
                                        start=True, stop=True)
                    ins.then_inc(done, 1)


_INS = ["x", "ctx_512", "g_xattn", "g_ffn", "L0_xattn_Wq", "L0_xattn_w_kc_q", "L0_xattn_w_kc_kv", "L0_xattn_W_qr",
        "L0_xattn_W_kr", "L0_xattn_Wo", "L0_ffn_in_gamma", "L0_ffn_in_beta", "L0_ffn_agg_w", "L0_ffn_agg_b",
        "L0_ffn_pn_gamma", "L0_ffn_pn_beta", "L0_ffn_d1_w", "L0_ffn_d1_b", "L0_ffn_d2_w", "L0_ffn_d2_b",
        "L0_ffn_bc_w", "L0_ffn_bc_b", "L0_ffn_gate_w", "L0_ffn_gate_b", "L0_ffn_out_gamma", "L0_ffn_out_beta"]


def shape_constants():
    import numpy as np

    f = np.float32
    inv_freq = (f(1.0) / f(10000.0) ** (np.arange(0, DC, 2, dtype=f) / f(DC))).astype(f)
    angle = np.arange(S, dtype=f)[:, None] * inv_freq[None, :]
    sin = np.repeat(np.sin(angle), 2, axis=-1).astype(f)
    cos = np.repeat(np.cos(angle), 2, axis=-1).astype(f)
    sin[:, :DC // 2] *= f(-1.0)

    def by_partition(table):
        return table.reshape(LB, P, DC).transpose(1, 0, 2).reshape(P, LB * DC)

    consts = np.concatenate([np.eye(P, dtype=f), by_partition(cos), by_partition(sin)], axis=1)
    row_pick = np.repeat(np.eye(NB, dtype=f)[:, :, None], P, axis=2)
    return {"consts": np.ascontiguousarray(consts), "row_pick": np.ascontiguousarray(row_pick)}


def kernel(**inputs):
    import numpy as np
    import concourse.bacc as bacc
    from concourse.bass_utils import run_bass_kernel_spmd

    nc = bacc.Bacc("TRN2", target_bir_lowering=False, num_devices=1)
    arrays, aps = {}, {}
    given = {name: np.ascontiguousarray(inputs[name]) for name in _INS}
    for name, a in {**given, **shape_constants()}.items():
        arrays[f"in_{name}"] = a
        aps[name] = nc.dram_tensor(f"in_{name}", a.shape, mybir.dt.from_np(a.dtype), kind="ExternalInput").ap()
    out = nc.dram_tensor("out_x", (NB, S, D), F32, kind="ExternalOutput").ap()
    gated_cross_attention_ffn(nc, aps, out)
    r = run_bass_kernel_spmd(nc, [arrays], core_ids=[0])
    return r.results[0]["out_x"]
```

```python
from contextlib import ExitStack

import concourse.bass as bass
from concourse import mybir

F32 = mybir.dt.float32
F32R = mybir.dt.float32r
BF16 = mybir.dt.bfloat16
ALU = mybir.AluOpType
ACT = mybir.ActivationFunctionType
AX = mybir.AxisListType

P = 128
NB, S, D = 4, 256, 256
H, K, DC, DCQ, R = 16, 128, 64, 192, 64
HID = 1024
STEPS = 4
NU = NB * S // P
KB = D // P
LB = S // P
HG = 4
NG = H // HG
JQ = DCQ // 2
HB = HID // P
EPS_BLOCK, EPS_FFN = 1e-5, 1e-6
PROBS_BUFS = 3
OUT_BUFS = 3
Y_BUFS = 2
W_CHUNKS = 8
PARTS = 3

UNIT_START = (0.23, 3.95, 7.94, 11.93, 15.85, 19.98, 24.02, 27.94)
FOLD_A_START, FOLD_B_START = (0.36, 1.47, 1.99, 3.0), (-1.46, 0.47, 1.35, 3.28)
ONCE = {
    "kv_rope": -6.85, "g_tanh": 0.89, ("wkrT", 0): -3.4, ("wkrT", 1): -3.45, ("kvT", 0): -2.4, ("kvT", 1): -1.66,
    ("vecT", 0): 1.76,
}
FOLD_A = {
    ("wkcqT", 0): -4.13, ("wkcqT", 1): -3.73, "qrT": -3.2, "qk": -2.45, "foldAT": -1.91, "foldA": -1.55, "gq": 0.51,
}
FOLD_B = {
    ("woT", 0): 0.53, ("woT", 1): 0.8, "foldB": 3.2,
}
FIRST_PAIR = {
    "x_stats": -23.23, "x_norm": -2.53, "xT": -0.19,
}
PAIR = {
    "x_stats": -8.31, "x_norm": -6.76, "xT": -3.9, "gq": -3.26,
}
GQ_PITCH = 1.1
SMAX_FIRST_PAIR, SMAX = (1.4, 1.41), (1.56, 1.92)
Q_HI_LOAD, SHIFT_T = 5.16, 5.43
SCORE_LAG = 7.0
AFTER = {
    "st": 0.04, "pv": 1.37, ("ctxT", 0): 4.31, ("ctxT", 1): 5.15, "out": 5.95, "y_norm": 6.3, "yT": 6.66,
    "gate": 7.56,
}
AFTER_LAST = {
    "st": 0.41, "pv": 1.47, ("ctxT", 0): 3.08, ("ctxT", 1): 5.2, "out": 5.82, "y_norm": 6.65, "yT": 8.14,
    "gate": 10.77,
}
LAST_PITCH = 0.77
W_PARTS_START, W_PARTS_PITCH = 8.36, 1.01
THOUGHT_START = 26.04
THOUGHT_PITCH = (0.34, 0.38, 0.35, 0.35, 0.23, 0.31, 1.1, 0.34, 0.27, 0.31, 1.06, 0.44,
                 0.28, 0.08, 0.95, 0.01, 0.28, 0.01, 0.34, 0.91, 0.01, 0.01)
FINAL_LAG = (13.75, 21.86, 13.65, 5.68, 16.68, 12.96, 11.12, 16.13)
FINAL_PITCH, FINAL_NORM = 0.8, 1.13
MOVED = {
    ("ctxT", 0): -0.05, ("ctxT", 1): -0.02, ("ctxT", 3): -0.09, ("ctxT", 6): -0.02, ("f_norm", 0): 0.04,
    ("f_norm", 1): -0.14, ("f_norm", 3): -0.04, ("f_norm", 4): 0.33, ("f_norm", 7): 0.35, ("f_pre", 1): 0.13,
    ("f_pre", 3): 0.16, ("f_pre", 6): -0.17, ("f_pre", 7): -0.16, ("foldA", 1): 0.03, ("foldA", 2): 0.52,
    ("foldA", 3): 0.29, ("foldAT", 1): -0.16, ("foldAT", 2): -0.54, ("foldAT", 3): -0.0, ("gate", 1): 0.33,
    ("gate", 2): 1.07, ("gate", 4): -0.17, ("gate", 5): 0.03, ("gate", 7): -1.09, ("gq", 1): 0.21, ("gq", 2): 0.04,
    ("gq", 3): -0.08, ("kvT", 0): 0.31, ("out", 0): -0.51, ("out", 4): -0.12, ("pv", 0): -0.08, ("pv", 1): 0.02,
    ("pv", 2): 0.03, ("pv", 3): -0.01, ("q_hi_load", 1): 0.23, ("q_hi_load", 2): -0.47, ("q_hi_load", 3): 0.14,
    ("q_hi_load", 5): -0.13, ("q_hi_load", 6): -0.4, ("q_hi_load", 7): -1.06, ("qk", 0): 0.1, ("qk", 1): -0.01,
    ("qk", 2): -0.14, ("qk", 3): 0.35, ("qrT", 0): 0.34, ("qrT", 3): 0.15, ("shiftT", 0): 0.09, ("shiftT", 3): 0.02,
    ("shiftT", 6): 0.01, ("shiftT", 7): 0.04, ("smax", 2): 0.32, ("smax", 6): -0.05, ("st", 0): 0.02,
    ("st", 1): -0.05, ("st", 2): -0.57, ("st", 3): 0.11, ("st", 5): 0.63, ("st", 7): 0.01, ("vecT", 0): 0.07,
    ("w_parts", 0): 0.09, ("w_parts", 1): -0.02, ("wkcqT", 0): 0.1, ("wkcqT", 1): -0.03, ("wkcqT", 2): 0.0,
    ("wkrT", 0): -0.01, ("wkrT", 1): 0.11, ("woT", 0): -0.14, ("woT", 1): -0.29, ("woT", 3): -0.05,
    ("woT", 6): 0.14, ("xT", 0): -0.27, ("xT", 1): -0.08, ("xT", 3): 0.05, ("x_norm", 2): -0.02,
    ("x_norm", 5): 0.34, ("x_norm", 6): -0.28, ("x_norm", 7): -0.03, ("x_stats", 0): -1.05, ("x_stats", 1): 0.0,
    ("x_stats", 2): -0.07, ("x_stats", 5): 0.06, ("x_stats", 7): 0.13, ("yT", 0): 0.27, ("yT", 1): 0.03,
    ("yT", 3): -0.04, ("yT", 5): 0.74, ("yT", 6): 0.28, ("y_norm", 1): 0.01, ("y_norm", 2): 0.01,
    ("y_norm", 3): -0.08, ("y_norm", 4): 0.15, ("y_norm", 6): -0.21, ("y_stats", 0): 0.13, ("y_stats", 1): 0.1,
}


def batch_of(u):
    return u % NB


def row_block_of(u):
    return 1 - u // NB


def thought_pieces():
    pieces = [[("c_stats", 0)], [("c_norm", 0), ("thoughtT", 0)], [("agg", 0), ("c_stats", 1)]]
    for k in range(STEPS):
        pieces += [[("c_norm", k + 1), ("thoughtT", k + 1)], [("up", k)], [("down", k)]]
        pieces += [[("downT", k)] + ([("c_stats", k + 2)] if k + 1 < STEPS else [])]
    return pieces + [[("thoughtT", STEPS + 1)], [("bc", 0)], [("bc_rows", 0), ("bc_rows", 1)]]


def make_plan():
    at = []

    def put(tick, *entry):
        at.append((tick + MOVED.get(entry[:2], 0), len(at), entry))

    for i in range(2):
        put(ONCE["wkrT", i], "wkrT", i)
    put(ONCE["kv_rope"], "kv_rope")
    put(ONCE["g_tanh"], "g_tanh")
    for i in range(2):
        put(ONCE["kvT", i], "kvT", i)
    put(ONCE["vecT", 0], "vecT", 0)
    for g in range(NG):
        for i in range(2):
            put(FOLD_A_START[g] + FOLD_A["wkcqT", i], "wkcqT", g, i)
        for name in ("qrT", "qk", "foldAT", "foldA"):
            put(FOLD_A_START[g] + FOLD_A[name], name, g)
        for i in range(2):
            put(FOLD_B_START[g] + FOLD_B["woT", i], "woT", 2 * g + i)
        put(FOLD_B_START[g] + FOLD_B["foldB"], "foldB", g)
    for U in range(NU // 2):
        start, pair = (UNIT_START[2 * U], PAIR) if U else (0, FIRST_PAIR)
        for u in (2 * U, 2 * U + 1):
            put(start + pair["x_stats"], "x_stats", u)
            put(start + pair["x_norm"], "x_norm", u)
        put(start + pair["xT"], "xT", U)
        for g in range(NG):
            put(start + g * GQ_PITCH + PAIR["gq"] if U else FOLD_A_START[g] + FOLD_A["gq"], "gq", U, g)
    for u in range(NU):
        for g in range(NG):
            for i in range(2):
                put(UNIT_START[u] + g + (SMAX if u > 1 else SMAX_FIRST_PAIR)[i], "smax", u, 2 * g + i)
        put(UNIT_START[u] + Q_HI_LOAD, "q_hi_load", u)
        put(UNIT_START[u] + SHIFT_T, "shiftT", u)
        start = UNIT_START[u] + SCORE_LAG
        after, pitch = (AFTER_LAST, LAST_PITCH) if u == NU - 1 else (AFTER, 1)
        for g in range(NG):
            put(start + g * pitch, "st", u, g, 0)
            put(start + g * pitch + after["st"], "st", u, g, 1)
            put(start + g * pitch + after["pv"], "pv", u, g)
        for i in range(2):
            put(start + after["ctxT", i], "ctxT", u, i)
        put(start + after["out"], "out", u)
        put(start + after["out"], "y_stats", u)
        for name in ("y_norm", "yT", "gate"):
            put(start + after[name], name, u)
    for i in range(2 * W_CHUNKS):
        put(W_PARTS_START + W_PARTS_PITCH * i, "w_parts", i // W_CHUNKS, i % W_CHUNKS)
    tick = THOUGHT_START
    for n, piece in enumerate(thought_pieces()):
        for entry in piece:
            put(tick, *entry)
        tick += THOUGHT_PITCH[n]
    for u in range(NU):
        tick = max(tick + FINAL_PITCH, UNIT_START[u] + SCORE_LAG + FINAL_LAG[u])
        put(tick, "f_pre", u)
        put(tick + FINAL_NORM, "f_norm", u)
    return [entry for _, _, entry in sorted(at)]


RINGS = {
    "max_ring": ("wkrT", "qk", "foldAT", "smax"),
    "score_ring": ("wkcqT", "woT", "st"),
    "ctx_ring": ("qrT", "foldB", "pv"),
    "misc_ring": ("kvT", "xT", "vecT", "foldA", "gq", "shiftT", "ctxT", "out", "yT", "gate", "thoughtT", "agg",
                  "up", "down", "downT", "bc", "bc_rows"),
}
SPLIT = ("kvT", "xT", "foldA", "foldB", "gq", "ctxT")
STATS = ("x_stats", "y_stats", "c_stats", "f_pre")


def gated_cross_attention_ffn(nc, t, out):
    plan = make_plan()
    place, turn = {}, {}
    for r, (ring, stages) in enumerate(RINGS.items()):
        for n, entry in enumerate(e for e in plan if e[0] in stages):
            place[entry], turn[entry] = 2 * r + n % 2, n // 2

    def nth(stages):
        return {e: n + 1 for n, e in enumerate(e for e in plan if e[0] in stages)}

    split_n = nth(SPLIT)
    stats_n = nth(STATS)
    x_norm_n, y_norm_n, c_norm_n = nth(("x_norm",)), nth(("y_norm",)), nth(("c_norm",))
    f_norm_n = nth(("f_norm",))
    job = {e: n - 1 for e, n in stats_n.items()}
    jobs = len(job)

    with ExitStack() as ctx:
        def sb(name, shape, dt=F32, stack=ctx):
            return stack.enter_context(nc.sbuf_tensor(name, shape, dt))

        def sem(name):
            return ctx.enter_context(nc.semaphore(name))

        ps = ctx.enter_context(nc.psum_tensor("ps", [P, 8, 512], F32))

        consts = sb("consts", [P, P + 2 * LB * DC])
        ident = consts[:, 0:P]
        rope_cos = consts[:, P:P + LB * DC].rearrange("p (l d) -> p l d", l=LB)
        rope_sin = consts[:, P + LB * DC:P + 2 * LB * DC].rearrange("p (l d) -> p l d", l=LB)
        kv1 = sb("kv1", [P, NB, LB, DC + 1])
        kv_hi2 = sb("kv_hi2", [P, NB, S], F32R)
        kv_lo = sb("kv_lo", [P, NB, S], F32R)
        x = sb("x", [P, NU, D])
        xn = sb("xn", [P, 2, D])
        y = sb("y", [P, Y_BUFS, D])
        xT_hi = sb("xT_hi", [P, KB, 2 * P], F32R)
        xT_lo = sb("xT_lo", [P, KB, 2 * P], F32R)
        A_hi = sb("A_hi", [P, KB, H * DC], F32R)
        A_lo = sb("A_lo", [P, KB, H * DC], F32R)
        B_hi = sb("B_hi", [P, H // 2, D], F32R)
        B_lo = sb("B_lo", [P, H // 2, D], F32R)
        agg_w = sb("agg_w", [P, KB, D])
        bc_w = sb("bc_w", [P, KB, D])
        gate_w = sb("gate_w", [P, KB, D])
        vec_rows = sb("vec_rows", [16, P])
        vecs = sb("vecs", [P, 16])
        agg_b = sb("agg_b", [NB, D])
        d2_b = sb("d2_b", [NB, D])
        bc_b = sb("bc_b", [NB, D])
        gate_b = sb("gate_b", [P, D])
        out_gamma = sb("out_gamma", [P, D])
        out_beta = sb("out_beta", [P, D])
        g_raw = sb("g_raw", [P, 2])
        g_tanh = sb("g_tanh", [P, 2])
        bn6 = sb("bn6", [P, 2, 6])
        mean_var = sb("mean_var", [P, jobs, 2])
        var_eps = sb("var_eps", [P, jobs])
        rstd = sb("rstd", [P, jobs])
        minus_half = sb("minus_half", [P, 1])
        row_max = sb("row_max", [P, 2, H])
        shift = sb("shift", [H, 2, P], F32R)
        prob_sum_inv = sb("prob_sum_inv", [P, HG])
        yT = sb("yT", [P, KB, P])
        last_rows = sb("last_rows", [NB, D])
        thought = sb("thought", [NB, D])
        thought_bias = sb("thought_bias", [NB, D])
        thought_norm = sb("thought_norm", [NB, D])
        thoughtT = sb("thoughtT", [P, KB, NB])
        thoughtT_rest = sb("thoughtT_rest", [P, KB, NB])
        thoughtT_parts = sb("thoughtT_parts", [P, KB, PARTS * NB], BF16)
        hid_sum = sb("hid_sum", [P, HB, NB])
        hid_in = sb("hid_in", [P, HB, NB])
        hid = sb("hid", [P, HB, NB])
        hid_rest = sb("hid_rest", [P, HB, NB])
        hid_parts = sb("hid_parts", [P, HB, PARTS * NB], BF16)
        down_sumT = sb("down_sumT", [P, KB, NB])
        bc4 = sb("bc4", [NB, D])
        q_split = [sb("q_split0", [P, H, 2 * P], F32R)]
        q_hi = sb("q_hi", [P, 2, H, P], F32R)

        stage = ExitStack()
        ctxt = sb("ctxt", [P, NB, LB, DC], F32, stage)
        rope_t = sb("rope_t", [P, LB, DC], F32, stage)
        wkr = sb("wkr", [P, H // 2, R], F32, stage)
        wkrT = sb("wkrT", [R, H * DC], F32, stage)
        wqr = sb("wqr", [JQ, H, 2, R], F32, stage)
        wkcq = sb("wkcq", [P, H, DCQ], F32, stage)
        wkcqT = sb("wkcqT", [JQ, 2, HG, 2, P], F32, stage)
        qrT = sb("qrT", [R, 2, HG * P], F32, stage)
        qk = sb("qk", [P, 2, HG * DC], F32, stage)
        AT = sb("AT", [P, 2, HG // 2, D], F32, stage)
        wq = sb("wq", [P, H, D], F32, stage)
        wo = sb("wo", [P, KB, H * K], F32, stage)
        wkckv = sb("wkckv", [P, H, DC], F32, stage)
        woT = sb("woT", [P, 4, 2, D], F32, stage)
        stage.close()
        q_split.append(sb("q_split1", [P, H, 2 * P], F32R))
        probs = sb("probs", [P, PROBS_BUFS, LB, HG * P])
        ctxn = sb("ctxn", [P, H * DC])
        ctxT_hi = sb("ctxT_hi", [P, H // 2, P], F32R)
        ctxT_lo = sb("ctxT_lo", [P, H // 2, P], F32R)
        gt = sb("gt", [P, NU, D])
        bc_all = sb("bc_all", [P, NB, D])
        fin = sb("fin", [P, OUT_BUFS, D])
        fin_in = sb("fin_in", [P, 2, D])
        row_pick = sb("row_pick", [NB, NB, P])
        w_rest = sb("w_rest", [P, KB * HID])
        d1_parts = sb("d1_parts", [P, PARTS, KB, HID], BF16)
        d2_parts = sb("d2_parts", [P, PARTS, HB, D], BF16)

        full = [sem(f"full{i}") for i in range(8)]
        free = [sem(f"free{i}") for i in range(8)]
        hi_done = sem("hi_done")
        ident_in, rope_in, ctx_in, row_pick_in = sem("ident_in"), sem("rope_in"), sem("ctx_in"), sem("row_pick_in")
        x_in = [sem(f"x_in{i}") for i in range(3)]
        wkr_in = sem("wkr_in")
        wqr_in = [sem(f"wqr_in{g}") for g in range(NG)]
        wkcq_in = [sem(f"wkcq_in{i}") for i in range(2 * NG)]
        wq_in = [sem(f"wq_in{g}") for g in range(NG)]
        wo_in = [sem(f"wo_in{i}") for i in range(2)]
        wkckv_in = sem("wkckv_in")
        vec_in, g_in, small_in = sem("vec_in"), sem("g_in"), sem("small_in")
        gate_w_in, agg_w_in, bc_w_in = sem("gate_w_in"), sem("agg_w_in"), sem("bc_w_in")
        d1_in, d2_in = sem("d1_in"), sem("d2_in")
        w_parts_made = sem("w_parts_made")
        kv_dup_in = sem("kv_dup_in")
        thought_parts_made, hid_parts_made = sem("thought_parts_made"), sem("hid_parts_made")
        q_hi_in = [sem(f"q_hi_in{i}") for i in range(2)]
        shift_in = [sem(f"shift_in{i}") for i in range(2)]
        last_in = [sem(f"last_in{b}") for b in range(NB)]
        stored = [sem(f"stored{i}") for i in range(OUT_BUFS)]
        kv_made = sem("kv_made")
        ones_row = sem("ones_row")
        q_hi_cleared = sem("q_hi_cleared")
        g_tanh_made = sem("g_tanh_made")
        out_scaled = sem("out_scaled")
        stats_made = sem("stats_made")
        rstd_made = sem("rstd_made")
        x_normed, y_normed, c_normed = sem("x_normed"), sem("y_normed"), sem("c_normed")
        gated = sem("gated")
        hid_in_made = sem("hid_in_made")
        gelu_made = sem("gelu_made")
        beta_added = sem("beta_added")
        fin_made = sem("fin_made")
        dve_chain, pool_chain = sem("dve_chain"), sem("pool_chain")

        def bank(e):
            return ps[:, place[e], :]

        def claim(pe, e):
            if turn[e]:
                pe.wait_ge(free[place[e]], turn[e])

        def filled(eng, e):
            eng.wait_ge(full[place[e]], turn[e] + 1)

        def taken(eng, e):
            eng.wait_ge(free[place[e]], turn[e] + 1)

        block = ctx.enter_context(nc.Block())

        @block.sync
        def _(sp):
            x_rows = t["x"].rearrange("b (q p) d -> q p b d", p=P)
            sp.dma_start(ident, t["consts"][:, 0:P]).then_inc(ident_in, 16)
            for g in range(NG):
                hs = slice(HG * g, HG * (g + 1))
                for i in range(2):
                    two = slice(HG * g + 2 * i, HG * g + 2 * i + 2)
                    sp.dma_start(wkcq[:, two, :], t["L0_xattn_w_kc_q"].rearrange("h k q -> k h q")[:, two, :]
                                 ).then_inc(wkcq_in[2 * g + i], 16)
                sp.dma_start(wqr[:, hs, :, :].rearrange("p h j r -> p h (j r)"),
                             t["L0_xattn_W_qr"].rearrange("h (p j) r -> p h (j r)", j=2)[:, hs, :]
                             ).then_inc(wqr_in[g], 16)
                if g == 0:
                    sp.dma_start(wkr[:, :, :], t["L0_xattn_W_kr"].rearrange("(g two) d r -> (two d) g r", two=2)
                                 ).then_inc(wkr_in, 16)
                sp.dma_start(wq[:, hs, :], t["L0_xattn_Wq"].rearrange("(h k) m -> k h m", k=K)[:, hs, :]
                             ).then_inc(wq_in[g], 16)
                if g == 0:
                    sp.dma_start(x[:, 0:2, :], x_rows[1][:, 0:2, :]).then_inc(x_in[0], 16)
                    sp.dma_start(consts[:, P:], t["consts"][:, P:]).then_inc(rope_in, 16)
                    sp.dma_start(ctxt[:, :, :, :], t["ctx_512"].rearrange("b (l p) d -> p b l d", p=P)
                                 ).then_inc(ctx_in, 16)
            sp.dma_start(x[:, 2:4, :], x_rows[1][:, 2:4, :]).then_inc(x_in[1], 16)
            for i in range(2):
                cols = slice(i * H * K // 2, (i + 1) * H * K // 2)
                sp.dma_start(wo[:, :, cols], t["L0_xattn_Wo"].rearrange("(b p) n -> p b n", p=P)[:, :, cols]
                             ).then_inc(wo_in[i], 16)
                if i == 0:
                    sp.dma_start(wkckv[:, :, :], t["L0_xattn_w_kc_kv"].rearrange("h k d -> k h d")
                                 ).then_inc(wkckv_in, 16)
            sp.dma_start(g_raw[:, 0:1], t["g_xattn"].partition_broadcast(P)).then_inc(g_in, 16)
            sp.dma_start(g_raw[:, 1:2], t["g_ffn"].partition_broadcast(P)).then_inc(g_in, 16)
            for i in range(2):
                sp.wait_ge(hi_done, split_n[("kvT", i)])
                sp.dma_start(kv_hi2[64:128, 2 * i:2 * i + 2, :].bitcast(F32),
                             kv_hi2[0:64, 2 * i:2 * i + 2, :].bitcast(F32)).then_inc(kv_dup_in, 16)
            sp.dma_start(x[:, NB:NU, :], x_rows[0]).then_inc(x_in[2], 16)
            sp.dma_start(out_gamma[:, :], t["L0_ffn_out_gamma"].partition_broadcast(P)).then_inc(small_in, 16)
            sp.dma_start(out_beta[:, :], t["L0_ffn_out_beta"].partition_broadcast(P)).then_inc(small_in, 16)
            sp.dma_start(gate_b[:, :], t["L0_ffn_gate_b"].partition_broadcast(P)).then_inc(small_in, 16)
            sp.dma_start(agg_b[:, :], t["L0_ffn_agg_b"].partition_broadcast(NB)).then_inc(small_in, 16)
            sp.dma_start(d2_b[:, :], t["L0_ffn_d2_b"].partition_broadcast(NB)).then_inc(small_in, 16)
            sp.dma_start(bc_b[:, :], t["L0_ffn_bc_b"].partition_broadcast(NB)).then_inc(small_in, 16)
            for i, name in enumerate(("in_gamma", "in_beta", "pn_gamma", "pn_beta")):
                sp.dma_start(vec_rows[2 * i:2 * i + 2, :], t["L0_ffn_" + name].rearrange("(b p) -> b p", p=P)
                             ).then_inc(vec_in, 16)
            sp.dma_start(vec_rows[8:16, :], t["L0_ffn_d1_b"].rearrange("(b p) -> b p", p=P)).then_inc(vec_in, 16)
            sp.dma_start(gate_w[:, :, :], t["L0_ffn_gate_w"].rearrange("(b p) n -> p b n", p=P)
                         ).then_inc(gate_w_in, 16)
            sp.dma_start(agg_w[:, :, :], t["L0_ffn_agg_w"].rearrange("(b p) n -> p b n", p=P)).then_inc(agg_w_in, 16)
            sp.dma_start(bc_w[:, :, :], t["L0_ffn_bc_w"].rearrange("(b p) n -> p b n", p=P)).then_inc(bc_w_in, 16)
            out_rows = out.rearrange("b (q p) d -> q p b d", p=P)
            for e in plan:
                if e == ("st", 0, 0, 0):
                    filled(sp, ("foldA", NG - 1))
                    filled(sp, ("foldB", NG - 1))
                    sp.dma_start(w_rest[:, :].rearrange("p (b n) -> p b n", b=KB),
                                 t["L0_ffn_d1_w"].rearrange("(b p) n -> p b n", p=P)).then_inc(d1_in, 16)
                    sp.dma_start(row_pick[:, :, :], t["row_pick"]).then_inc(row_pick_in, 16)
                if e == ("w_parts", 1, 0):
                    sp.wait_ge(w_parts_made, W_CHUNKS)
                    sp.dma_start(w_rest[:, :].rearrange("p (b n) -> p b n", b=HB),
                                 t["L0_ffn_d2_w"].rearrange("(b p) n -> p b n", p=P)).then_inc(d2_in, 16)
                if e[0] == "q_hi_load":
                    u = e[1]
                    sp.wait_ge(hi_done, split_n[("gq", u // 2, NG - 1)])
                    if u >= 2:
                        filled(sp, ("st", u - 2, NG - 1, 1))
                    for odd in range(2):
                        src = q_split[u // 2 % 2][64 * odd:64 * odd + 64, :, u % 2 * P:u % 2 * P + P]
                        src = src.rearrange("p (g two) q -> p g two q", two=2)[:, :, odd, :]
                        dst = q_hi[0:64, u % 2, :, :].rearrange("p (g two) q -> p g two q", two=2)[:, :, odd, :]
                        sp.dma_start(dst.bitcast(F32), src.bitcast(F32)).then_inc(q_hi_in[u % 2], 16)
                if e[0] == "shiftT":
                    s = e[1]
                    taken(sp, e)
                    if s == 0:
                        sp.wait_ge(q_hi_cleared, 1)
                    sp.dma_start(q_hi[64:65, s % 2, :, :].bitcast(F32),
                                 shift[:, s % 2, :].bitcast(F32)
                                 ).then_inc(shift_in[s % 2], 16)
                if e[0] == "y_norm" and e[1] < NB:
                    sp.wait_ge(y_normed, y_norm_n[e])
                    sp.dma_start(last_rows[e[1]:e[1] + 1, :], y[P - 1:P, e[1] % Y_BUFS, :]).then_inc(last_in[e[1]], 16)
                if e[0] == "f_norm":
                    u, n = e[1], f_norm_n[e]
                    sp.wait_ge(fin_made, n)
                    sp.dma_start(out_rows[row_block_of(u)][:, batch_of(u), :], fin[:, (n - 1) % OUT_BUFS, :]
                                 ).then_inc(stored[(n - 1) % OUT_BUFS], 16)
            for i in range(OUT_BUFS):
                sp.wait_ge(stored[i], 16 * len(range(i, NU, OUT_BUFS)))

        @block.gpsimd
        def _(pool):
            chained = [0]

            def link(ins):
                chained[0] += 1
                ins.then_inc(pool_chain, 1)
                pool.wait_ge(pool_chain, chained[0])

            link(pool.memset(minus_half[:, :], -0.5))
            link(pool.memset(kv1[:, :, :, DC:DC + 1], 1.0))
            pool.memset(q_hi[64:P, :, :, :].bitcast(F32), 0.0).then_inc(q_hi_cleared, 1)
            pool.wait_ge(q_hi_cleared, 1)
            for e in plan:
                if e[0] == "kv_rope":
                    pool.wait_ge(rope_in, 16)
                    pool.wait_ge(ctx_in, 16)
                    half = DC // 2
                    for b in range(NB):
                        kv = kv1[:, b, :, 0:DC]
                        pool.tensor_tensor(kv, ctxt[:, b], rope_cos, ALU.mult)
                        pool.tensor_tensor(rope_t[:, :, 0:half], ctxt[:, b, :, half:DC], rope_sin[:, :, 0:half],
                                           ALU.mult)
                        link(pool.tensor_tensor(rope_t[:, :, half:DC], ctxt[:, b, :, 0:half],
                                                rope_sin[:, :, half:DC], ALU.mult))
                        pool.tensor_tensor(kv, kv, rope_t[:, :, :], ALU.add).then_inc(kv_made, 1)
                        pool.wait_ge(kv_made, b + 1)
                if e[0] in STATS:
                    n = job[e]
                    rows = NB if e[0] == "c_stats" else P
                    eps = EPS_FFN if e[0] in ("c_stats", "f_pre") else EPS_BLOCK
                    pool.wait_ge(stats_made, stats_n[e])
                    link(pool.tensor_scalar(var_eps[0:rows, n:n + 1], mean_var[0:rows, n, 1:2], eps, None, ALU.add))
                    pool.tensor_tensor(rstd[0:rows, n:n + 1], var_eps[0:rows, n:n + 1], minus_half[0:rows, :],
                                       ALU.pow).then_inc(rstd_made, 1)
                if e[0] == "w_parts":
                    _, i, c = e
                    pool.wait_ge(d2_in if i else d1_in, 16)
                    cols = slice(c * KB * HID // W_CHUNKS, (c + 1) * KB * HID // W_CHUNKS)
                    parts = (d2_parts if i else d1_parts)[:, :, :, :].rearrange("p i b n -> p i (b n)")[:, :, cols]
                    link(pool.tensor_copy(parts[:, 0, :], w_rest[:, cols]))
                    link(pool.tensor_tensor(w_rest[:, cols], w_rest[:, cols], parts[:, 0, :], ALU.subtract))
                    link(pool.tensor_copy(parts[:, 1, :], w_rest[:, cols]))
                    pool.tensor_tensor(parts[:, 2, :], w_rest[:, cols], parts[:, 1, :], ALU.subtract
                                       ).then_inc(w_parts_made, 1)
                if e == ("out", 0):
                    pool.wait_ge(g_tanh_made, 1)
                    pool.wait_ge(small_in, 16 * 6)
                    pool.tensor_scalar(out_gamma[:, :], out_gamma[:, :], g_tanh[:, 1:2], None, ALU.mult
                                       ).then_inc(out_scaled, 1)
                    link(pool.tensor_scalar(out_beta[:, :], out_beta[:, :], g_tanh[:, 1:2], None, ALU.mult))
                if e[0] == "f_pre":
                    pool.tensor_tensor(x[:, e[1], :], x[:, e[1], :], out_beta[:, :], ALU.add).then_inc(beta_added, 1)

        @block.scalar
        def _(act):
            for e in plan:
                name = e[0]
                if name == "g_tanh":
                    act.wait_ge(g_in, 32)
                    act.activation(g_tanh[:, :], g_raw[:, :], ACT.Tanh).then_inc(g_tanh_made, 1)
                if name == "kvT":
                    filled(act, e)
                    bs = slice(2 * e[1], 2 * e[1] + 2)
                    act.activation(kv_hi2[0:64, bs, :].rearrange("p b l -> p (b l)"), bank(e)[0:64, :], ACT.Copy
                                   ).then_inc(hi_done, 1)
                if name == "xT":
                    filled(act, e)
                    act.activation(xT_hi[:, :, :].rearrange("p k q -> p (k q)"), bank(e), ACT.Copy
                                   ).then_inc(hi_done, 1)
                if name == "wkrT":
                    filled(act, e)
                    act.activation(wkrT[:, 512 * e[1]:512 * e[1] + 512], bank(e)[0:R, :], ACT.Copy
                                   ).then_inc(free[place[e]], 1)
                if name == "wkcqT" and e[2] == 0:
                    filled(act, e)
                    act.activation(wkcqT[:, e[1] % 2, 0:2].rearrange("p h j k -> p (h j k)"), bank(e)[0:JQ, :],
                                   ACT.Copy).then_inc(free[place[e]], 1)
                if name == "qk":
                    filled(act, e)
                    act.activation(qk[:, e[1] % 2, :], bank(e)[:, 0:HG * DC], ACT.Copy).then_inc(free[place[e]], 1)
                if name == "foldAT":
                    filled(act, e)
                    act.activation(AT[:, e[1] % 2].rearrange("p g m -> p (g m)"), bank(e), ACT.Copy
                                   ).then_inc(free[place[e]], 1)
                if name == "foldA":
                    filled(act, e)
                    cols = slice(HG * DC * e[1], HG * DC * (e[1] + 1))
                    act.activation(A_hi[:, :, cols], bank(e).rearrange("p (k n) -> p k n", k=KB), ACT.Copy
                                   ).then_inc(hi_done, 1)
                if name == "woT" and e[1] % 2 == 0:
                    filled(act, e)
                    act.activation(woT[:, e[1] % 4].rearrange("p h m -> p (h m)"), bank(e), ACT.Copy
                                   ).then_inc(free[place[e]], 1)
                if name == "foldB":
                    filled(act, e)
                    act.activation(B_hi[:, 2 * e[1]:2 * e[1] + 2, :].rearrange("p g m -> p (g m)"), bank(e), ACT.Copy
                                   ).then_inc(hi_done, 1)
                if name == "gq":
                    _, U, j = e
                    dst = q_split[U % 2][:, HG * j:HG * j + HG, :].rearrange("p (g two) q -> p g two q", two=2)
                    src = bank(e).rearrange("p (g q) -> p g q", g=2)
                    filled(act, e)
                    act.activation(dst[0:64, :, 0, :], src[0:64], ACT.Copy)
                    act.activation(dst[64:128, :, 1, :], src[64:128], ACT.Copy).then_inc(hi_done, 1)
                if name == "shiftT":
                    filled(act, e)
                    act.activation(shift[:, e[1] % 2, :], bank(e)[0:H, 0:P], ACT.Copy, scale=-1.0
                                   ).then_inc(free[place[e]], 1)
                if name == "st":
                    _, u, g, lb = e
                    n = u * NG + g
                    if n >= PROBS_BUFS:
                        m = n - PROBS_BUFS
                        filled(act, ("pv", m // NG, m % NG))
                    filled(act, e)
                    act.activation(probs[:, n % PROBS_BUFS, lb, :], bank(e), ACT.Exp).then_inc(free[place[e]], 1)
                if name == "ctxT":
                    filled(act, e)
                    act.activation(ctxT_hi[:, 4 * e[2]:4 * e[2] + 4, :].rearrange("p g q -> p (g q)"), bank(e),
                                   ACT.Copy).then_inc(hi_done, 1)
                if name == "yT":
                    filled(act, e)
                    act.activation(yT[:, :, :].rearrange("p k q -> p (k q)"), bank(e)[:, 0:KB * P], ACT.Copy
                                   ).then_inc(free[place[e]], 1)
                if name == "gate":
                    u = e[1]
                    taken(act, e)
                    act.activation(gt[:, u, :], gt[:, u, :], ACT.Tanh, scale=0.5).then_inc(gated, 1)
                if name == "up":
                    act.wait_ge(hid_in_made, e[1] + 1)
                    act.activation(hid[:, :, :], hid_in[:, :, :], ACT.Gelu).then_inc(gelu_made, 1)
                if name == "bc_rows":
                    filled(act, e)
                    act.activation(bc_all[:, 2 * e[1]:2 * e[1] + 2, :].rearrange("p b d -> p (b d)"), bank(e),
                                   ACT.Copy).then_inc(free[place[e]], 1)

        @block.vector
        def _(dve):
            chained = [0]

            def link(ins):
                chained[0] += 1
                ins.then_inc(dve_chain, 1)
                dve.wait_ge(dve_chain, chained[0])

            def stats(rows, src, e):
                if stats_n[e] > 1:
                    dve.wait_ge(stats_made, stats_n[e] - 1)
                link(dve.bn_stats(bn6[0:rows, 0, :], src))
                dve.bn_aggr(mean_var[0:rows, job[e], :], bn6[0:rows, 0, :]).then_inc(stats_made, 1)

            def normalise(rows, dst, src, e):
                n = job[e]
                dve.wait_ge(rstd_made, stats_n[e])
                return dve.tensor_scalar(dst, src, mean_var[0:rows, n, 0:1], rstd[0:rows, n:n + 1], ALU.subtract,
                                         ALU.mult)

            def bf16_parts(parts, rest, src):
                link(dve.tensor_copy(parts[:, :, 0:NB], src))
                link(dve.tensor_tensor(rest, src, parts[:, :, 0:NB], ALU.subtract))
                link(dve.tensor_copy(parts[:, :, NB:2 * NB], rest))
                return dve.tensor_tensor(parts[:, :, 2 * NB:3 * NB], rest, parts[:, :, NB:2 * NB], ALU.subtract)

            link(dve.memset(kv_lo[64:P, :, :].bitcast(F32), 0.0))
            dve.memset(kv_lo[64:65, :, :].bitcast(F32), 1.0).then_inc(ones_row, 1)
            for e in plan:
                name = e[0]
                if name == "x_stats":
                    u = e[1]
                    if u % NB % 2 == 0:
                        dve.wait_ge(x_in[min(u // 2, 2)], 16)
                    stats(P, x[:, u, :], e)
                if name == "x_norm":
                    u = e[1]
                    normalise(P, xn[:, u % 2, :], x[:, u, :], ("x_stats", u)).then_inc(x_normed, 1)
                if name == "kvT":
                    dve.wait_ge(hi_done, split_n[e])
                    bs = slice(2 * e[1], 2 * e[1] + 2)
                    dve.tensor_tensor(kv_lo[0:64, bs, :].rearrange("p b l -> p (b l)"), bank(e)[0:64, :],
                                      kv_hi2[0:64, bs, :].rearrange("p b l -> p (b l)").bitcast(F32), ALU.subtract
                                      ).then_inc(free[place[e]], 1)
                if name == "xT":
                    dve.wait_ge(hi_done, split_n[e])
                    dve.tensor_tensor(xT_lo[:, :, :].rearrange("p k q -> p (k q)"), bank(e),
                                      xT_hi[:, :, :].rearrange("p k q -> p (k q)").bitcast(F32), ALU.subtract
                                      ).then_inc(free[place[e]], 1)
                if name == "wkcqT" and e[2] == 1:
                    filled(dve, e)
                    dve.tensor_copy(wkcqT[:, e[1] % 2, 2:4].rearrange("p h j k -> p (h j k)"), bank(e)[0:JQ, :]
                                    ).then_inc(free[place[e]], 1)
                if name == "qrT":
                    filled(dve, e)
                    dve.tensor_copy(qrT[:, e[1] % 2, :], bank(e)[0:R, :]).then_inc(free[place[e]], 1)
                if name == "foldA":
                    dve.wait_ge(hi_done, split_n[e])
                    cols = slice(HG * DC * e[1], HG * DC * (e[1] + 1))
                    dve.tensor_tensor(A_lo[:, :, cols], bank(e).rearrange("p (k n) -> p k n", k=KB),
                                      A_hi[:, :, cols].bitcast(F32), ALU.subtract).then_inc(free[place[e]], 1)
                if name == "woT" and e[1] % 2 == 1:
                    filled(dve, e)
                    dve.tensor_copy(woT[:, e[1] % 4].rearrange("p h m -> p (h m)"), bank(e)
                                    ).then_inc(free[place[e]], 1)
                if name == "foldB":
                    dve.wait_ge(hi_done, split_n[e])
                    gs = slice(2 * e[1], 2 * e[1] + 2)
                    dve.tensor_tensor(B_lo[:, gs, :].rearrange("p g m -> p (g m)"), bank(e),
                                      B_hi[:, gs, :].rearrange("p g m -> p (g m)").bitcast(F32), ALU.subtract
                                      ).then_inc(free[place[e]], 1)
                if name == "vecT":
                    filled(dve, e)
                    dve.tensor_copy(vecs[:, :], bank(e)[:, 0:16]).then_inc(free[place[e]], 1)
                if name == "gq":
                    _, U, j = e
                    dst = q_split[U % 2][:, HG * j:HG * j + HG, :].rearrange("p (g two) q -> p g two q", two=2)
                    src = bank(e).rearrange("p (g q) -> p g q", g=2)
                    dve.wait_ge(hi_done, split_n[e])
                    dve.tensor_tensor(dst[64:128, :, 0, :], src[0:64], dst[0:64, :, 0, :].bitcast(F32), ALU.subtract)
                    dve.tensor_tensor(dst[0:64, :, 1, :], src[64:128], dst[64:128, :, 1, :].bitcast(F32), ALU.subtract
                                      ).then_inc(free[place[e]], 1)
                if name == "smax":
                    _, s, j = e
                    filled(dve, e)
                    dve.reduce_max(row_max[:, s % 2, 2 * j:2 * j + 2], bank(e).rearrange("p (h l) -> p h l", h=2), AX.X
                                   ).then_inc(free[place[e]], 1)
                if name == "pv":
                    _, u, g = e
                    if (u, g) != (0, 0):
                        taken(dve, ("pv", u, g - 1) if g else ("pv", u - 1, NG - 1))
                    filled(dve, e)
                    r = bank(e)[:, 0:HG * (DC + 1)].rearrange("p (h d) -> p h d", h=HG)
                    link(dve.reciprocal(prob_sum_inv[:, :].unsqueeze(2), r[:, :, DC:DC + 1]))
                    dve.tensor_tensor(ctxn[:, HG * DC * g:HG * DC * (g + 1)].rearrange("p (h d) -> p h d", h=HG),
                                      r[:, :, 0:DC], prob_sum_inv[:, :].unsqueeze(2).to_broadcast([P, HG, DC]),
                                      ALU.mult).then_inc(free[place[e]], 1)
                if name == "ctxT":
                    gs = slice(4 * e[2], 4 * e[2] + 4)
                    dve.wait_ge(hi_done, split_n[e])
                    dve.tensor_tensor(ctxT_lo[:, gs, :].rearrange("p g q -> p (g q)"), bank(e),
                                      ctxT_hi[:, gs, :].rearrange("p g q -> p (g q)").bitcast(F32), ALU.subtract
                                      ).then_inc(free[place[e]], 1)
                if name == "out":
                    u = e[1]
                    if u == 0:
                        dve.wait_ge(g_tanh_made, 1)
                    filled(dve, e)
                    ins = dve.scalar_tensor_tensor(x[:, u, :], bank(e)[:, 0:D], g_tanh[:, 0:1], x[:, u, :], ALU.mult,
                                                   ALU.add)
                    ins.then_inc(free[place[e]], 1)
                    taken(dve, e)
                if name == "y_stats":
                    stats(P, x[:, e[1], :], e)
                if name == "y_norm":
                    u = e[1]
                    if Y_BUFS <= u < NB + Y_BUFS:
                        dve.wait_ge(last_in[u - Y_BUFS], 16)
                    normalise(P, y[:, u % Y_BUFS, :], x[:, u, :], ("y_stats", u)).then_inc(y_normed, 1)
                if name == "gate":
                    if e[1] == 0:
                        dve.wait_ge(small_in, 16 * 6)
                    filled(dve, e)
                    dve.tensor_tensor(gt[:, e[1], :], bank(e)[:, 0:D], gate_b[:, :], ALU.add
                                      ).then_inc(free[place[e]], 1)
                if name == "c_stats":
                    if e[1] == 0:
                        for b in range(NB):
                            dve.wait_ge(last_in[b], 16)
                    stats(NB, (last_rows if e[1] == 0 else thought)[:, :], e)
                if name == "c_norm":
                    k = e[1]
                    normalise(NB, thought_norm[:, :], (last_rows if k == 0 else thought)[:, :], ("c_stats", k)
                              ).then_inc(c_normed, 1)
                    if k:
                        link(dve.tensor_tensor(thought_bias[:, :], thought[:, :], d2_b[:, :], ALU.add))
                if name == "thoughtT":
                    k = e[1]
                    filled(dve, e)
                    cols = bank(e)[:, 0:KB * NB].rearrange("p (k b) -> p k b", k=KB)
                    if k == STEPS + 1:
                        dve.tensor_copy(thoughtT[:, :, :], cols).then_inc(free[place[e]], 1)
                    else:
                        c = 0 if k == 0 else 4
                        for kb in range(KB):
                            ins = dve.tensor_scalar(thoughtT[:, kb, :], cols[:, kb, :], vecs[:, c + kb:c + kb + 1],
                                                    vecs[:, c + KB + kb:c + KB + kb + 1], ALU.mult, ALU.add)
                        ins.then_inc(free[place[e]], 1)
                    if 1 <= k <= STEPS:
                        taken(dve, e)
                        bf16_parts(thoughtT_parts, thoughtT_rest[:, :, :], thoughtT[:, :, :]
                                   ).then_inc(thought_parts_made, 1)
                if name == "agg":
                    filled(dve, e)
                    dve.tensor_tensor(thought[:, :], bank(e)[0:NB, 0:D], agg_b[:, :], ALU.add
                                      ).then_inc(free[place[e]], 1)
                    taken(dve, e)
                if name == "up":
                    filled(dve, e)
                    parts = bank(e)[:, 0:HB * PARTS * NB].rearrange("p (j i b) -> p j b i", j=HB, i=PARTS)
                    dve.tensor_reduce(hid_sum[:, :, :], parts, AX.X, ALU.add).then_inc(free[place[e]], 1)
                    taken(dve, e)
                    dve.tensor_tensor(hid_in[:, :, :], hid_sum[:, :, :],
                                      vecs[:, 8:8 + HB].unsqueeze(2).to_broadcast([P, HB, NB]), ALU.add
                                      ).then_inc(hid_in_made, 1)
                if name == "down":
                    dve.wait_ge(gelu_made, e[1] + 1)
                    bf16_parts(hid_parts, hid_rest[:, :, :], hid[:, :, :]).then_inc(hid_parts_made, 1)
                    filled(dve, e)
                    parts = bank(e)[:, 0:KB * PARTS * NB].rearrange("p (k i b) -> p k b i", k=KB, i=PARTS)
                    dve.tensor_reduce(down_sumT[:, :, :], parts, AX.X, ALU.add).then_inc(free[place[e]], 1)
                if name == "downT":
                    filled(dve, e)
                    dve.tensor_tensor(thought[:, :], bank(e)[0:NB, 0:D], thought_bias[:, :], ALU.add
                                      ).then_inc(free[place[e]], 1)
                    taken(dve, e)
                if name == "bc":
                    filled(dve, e)
                    link(dve.tensor_tensor(bc4[:, :], bank(e)[0:NB, 0:D], bc_b[:, :], ALU.add))
                    dve.tensor_scalar(bc4[:, :], bc4[:, :], 0.5, None, ALU.mult).then_inc(free[place[e]], 1)
                if name == "f_pre":
                    u = e[1]
                    if u >= 2:
                        dve.wait_ge(fin_made, u - 1)
                    normalise(P, fin_in[:, u % 2, :], x[:, u, :], ("y_stats", u)).then_inc(dve_chain, 1)
                    chained[0] += 1
                    dve.wait_ge(gated, u + 1)
                    if u == 0:
                        dve.wait_ge(out_scaled, 1)
                        for i in range(2):
                            taken(dve, ("bc_rows", i))
                    link(dve.scalar_tensor_tensor(gt[:, u, :], gt[:, u, :], 1.0, bc_all[:, batch_of(u), :], ALU.add,
                                                  ALU.mult))
                    link(dve.tensor_tensor(fin_in[:, u % 2, :], fin_in[:, u % 2, :], gt[:, u, :], ALU.add))
                    stats(P, fin_in[:, u % 2, :], e)
                if name == "f_norm":
                    u, n = e[1], f_norm_n[e]
                    if n > OUT_BUFS:
                        dve.wait_ge(stored[(n - 1) % OUT_BUFS], 16 * ((n - 1) // OUT_BUFS))
                    f, i = fin[:, (n - 1) % OUT_BUFS, :], job[("f_pre", u)]
                    dve.wait_ge(stats_made, stats_n[("f_pre", u)])
                    link(dve.scalar_tensor_tensor(f, fin_in[:, u % 2, :], mean_var[:, i, 0:1], out_gamma[:, :],
                                                  ALU.subtract, ALU.mult))
                    dve.wait_ge(rstd_made, stats_n[("f_pre", u)])
                    dve.wait_ge(beta_added, u + 1)
                    dve.scalar_tensor_tensor(f, f, rstd[:, i:i + 1], x[:, u, :], ALU.mult, ALU.add
                                             ).then_inc(fin_made, 1)

        @block.tensor
        def _(pe):
            def split_product(dst, a_hi, a_lo, b_hi, b_lo, first, last):
                pe.matmul(dst, a_hi, b_lo, start=first, stop=False)
                pe.matmul(dst, a_hi, b_hi, start=False, stop=False)
                return pe.matmul(dst, a_lo, b_hi, start=False, stop=last)

            for e in plan:
                name = e[0]
                done = full[place[e]] if e in place else None
                if e in place:
                    claim(pe, e)
                if name == "kvT":
                    pe.wait_ge(kv_made, 2 * e[1] + 2)
                    for i in range(2 * LB):
                        b, lb = 2 * e[1] + i // LB, i % LB
                        ins = pe.transpose(bank(e)[0:DC, i * P:(i + 1) * P], kv1[:, b, lb, 0:DC], ident)
                    ins.then_inc(done, 1)
                if name == "xT":
                    U = e[1]
                    pe.wait_ge(x_normed, 2 * U + 2)
                    for kb in range(KB):
                        for i in range(2):
                            ins = pe.transpose(bank(e)[:, kb * 2 * P + i * P:kb * 2 * P + (i + 1) * P],
                                               xn[:, i, kb * P:(kb + 1) * P], ident)
                    ins.then_inc(done, 1)
                if name == "wkrT":
                    pe.wait_ge(wkr_in, 16)
                    for i in range(4):
                        ins = pe.transpose(bank(e)[0:R, i * P:(i + 1) * P], wkr[:, 4 * e[1] + i, :], ident)
                    ins.then_inc(done, 1)
                if name == "wkcqT":
                    _, g, i = e
                    pe.wait_ge(wkcq_in[2 * g + i], 16)
                    if g == 0 and i == 0:
                        pe.wait_ge(ident_in, 16)
                    for hh in range(2):
                        for j in range(2):
                            c = (2 * hh + j) * P
                            ins = pe.transpose(bank(e)[0:JQ, c:c + P], wkcq[:, HG * g + 2 * i + hh, j:DCQ:2], ident)
                    ins.then_inc(done, 1)
                if name == "qrT":
                    g = e[1]
                    pe.wait_ge(wqr_in[g], 16)
                    taken(pe, ("wkcqT", g, 0))
                    taken(pe, ("wkcqT", g, 1))
                    for hh in range(HG):
                        for j in range(2):
                            ins = pe.matmul(bank(e)[0:R, hh * P:(hh + 1) * P], wqr[:, HG * g + hh, j, :],
                                            wkcqT[:, g % 2, hh, j, :], start=(j == 0), stop=(j == 1))
                    ins.then_inc(done, 1)
                if name == "qk":
                    g = e[1]
                    taken(pe, ("qrT", g))
                    if g == 0:
                        taken(pe, ("wkrT", 0))
                        taken(pe, ("wkrT", 1))
                    for hh in range(HG):
                        h = HG * g + hh
                        ins = pe.matmul(bank(e)[:, hh * DC:(hh + 1) * DC], qrT[:, g % 2, hh * P:(hh + 1) * P],
                                        wkrT[:, h * DC:(h + 1) * DC], start=True, stop=True)
                    ins.then_inc(done, 1)
                if name == "foldAT":
                    g = e[1]
                    pe.wait_ge(wq_in[g], 16)
                    taken(pe, ("qk", g))
                    for hh in range(HG):
                        ins = pe.matmul(bank(e)[64 * (hh % 2):64 * (hh % 2) + 64, hh // 2 * D:(hh // 2 + 1) * D],
                                        qk[:, g % 2, hh * DC:(hh + 1) * DC], wq[:, HG * g + hh, :],
                                        start=True, stop=True)
                    ins.then_inc(done, 1)
                if name == "foldA":
                    g = e[1]
                    taken(pe, ("foldAT", g))
                    for kb in range(KB):
                        for i in range(2):
                            c = kb * HG * DC + i * P
                            ins = pe.transpose(bank(e)[:, c:c + P], AT[:, g % 2, i, kb * P:(kb + 1) * P], ident)
                    ins.then_inc(done, 1)
                if name == "woT":
                    i = e[1]
                    pe.wait_ge(wo_in[i // 4], 16)
                    for hh in range(2):
                        for kb in range(KB):
                            c = hh * D + kb * P
                            h = 2 * i + hh
                            ins = pe.transpose(bank(e)[:, c:c + P], wo[:, kb, h * K:(h + 1) * K], ident)
                    ins.then_inc(done, 1)
                if name == "foldB":
                    i = e[1]
                    pe.wait_ge(wkckv_in, 16)
                    taken(pe, ("woT", 2 * i))
                    taken(pe, ("woT", 2 * i + 1))
                    for hh in range(HG):
                        h = HG * i + hh
                        ins = pe.matmul(bank(e)[64 * (hh % 2):64 * (hh % 2) + 64, hh // 2 * D:(hh // 2 + 1) * D],
                                        wkckv[:, h, :], woT[:, h // 2 % 4, hh % 2, :], start=True, stop=True)
                    ins.then_inc(done, 1)
                if name == "vecT":
                    pe.wait_ge(vec_in, 16 * 5)
                    pe.transpose(bank(e)[:, 0:16], vec_rows[:, :], ident[0:16, 0:16]).then_inc(done, 1)
                if name == "gq":
                    _, U, j = e
                    taken(pe, ("foldA", j))
                    taken(pe, ("xT", U))
                    for i in range(2):
                        c = (2 * j + i) * P
                        for kb in range(KB):
                            ins = split_product(bank(e)[:, i * 2 * P:(i + 1) * 2 * P], A_hi[:, kb, c:c + P],
                                                A_lo[:, kb, c:c + P], xT_hi[:, kb, :], xT_lo[:, kb, :],
                                                kb == 0, kb == KB - 1)
                    ins.then_inc(done, 1)
                if name == "smax":
                    _, s, j = e
                    if j == 0 and s == 0:
                        taken(pe, ("kvT", 0))
                        taken(pe, ("kvT", 1))
                        pe.wait_ge(kv_dup_in, 32)
                    if s % 2 == 0 and j % 2 == 0:
                        taken(pe, ("gq", s // 2, j // 2))
                    for i in range(2):
                        ins = pe.matmul(bank(e)[:, i * S:(i + 1) * S],
                                        q_split[s // 2 % 2][:, 2 * j + i, s % 2 * P:s % 2 * P + P],
                                        kv_hi2[:, batch_of(s), :], start=True, stop=True)
                    ins.then_inc(done, 1)
                if name == "shiftT":
                    s = e[1]
                    taken(pe, ("smax", s, 6))
                    taken(pe, ("smax", s, 7))
                    pe.transpose(bank(e)[0:H, 0:P], row_max[:, s % 2, :], ident).then_inc(done, 1)
                if name == "st":
                    _, u, g, lb = e
                    U = u // 2
                    q = slice(u % 2 * P, u % 2 * P + P)
                    hs = slice(HG * g, HG * (g + 1))
                    if g == 0 and lb == 0:
                        pe.wait_ge(q_hi_in[u % 2], 32 * (u // 2 + 1))
                        pe.wait_ge(shift_in[u % 2], 16 * (u // 2 + 1))
                        if u == 0:
                            pe.wait_ge(ones_row, 1)
                    dst = bank(e).rearrange("p (h q) -> p h q", h=HG)
                    pe.matmul(dst, kv_lo[:, batch_of(u), lb * P:(lb + 1) * P], q_hi[:, u % 2, hs, :],
                              start=True, stop=False)
                    pe.matmul(dst, kv_hi2[:, batch_of(u), lb * P:(lb + 1) * P], q_split[U % 2][:, hs, q],
                              start=False, stop=True).then_inc(done, 1)
                if name == "pv":
                    _, u, g = e
                    n = u * NG + g
                    taken(pe, ("st", u, g, LB - 1))
                    taken(pe, ("st", u, g, 0))
                    for hh in range(HG):
                        for lb in range(LB):
                            ins = pe.matmul(bank(e)[:, hh * (DC + 1):(hh + 1) * (DC + 1)],
                                            probs[:, n % PROBS_BUFS, lb, hh * P:(hh + 1) * P],
                                            kv1[:, batch_of(u), lb, :], start=(lb == 0), stop=(lb == LB - 1))
                    ins.then_inc(done, 1)
                if name == "ctxT":
                    _, u, half = e
                    taken(pe, ("pv", u, 2 * half))
                    taken(pe, ("pv", u, 2 * half + 1))
                    for i in range(4):
                        c = (4 * half + i) * P
                        ins = pe.transpose(bank(e)[:, i * P:(i + 1) * P], ctxn[:, c:c + P], ident)
                    ins.then_inc(done, 1)
                if name == "out":
                    u = e[1]
                    if u == 0:
                        for i in range(NG):
                            taken(pe, ("foldB", i))
                    for i in range(H // 2):
                        if i % 4 == 0:
                            taken(pe, ("ctxT", u, i // 4))
                        ins = split_product(bank(e)[:, 0:D], ctxT_hi[:, i, :], ctxT_lo[:, i, :], B_hi[:, i, :],
                                            B_lo[:, i, :], i == 0, i == H // 2 - 1)
                    ins.then_inc(done, 1)
                if name == "yT":
                    u = e[1]
                    pe.wait_ge(y_normed, y_norm_n[("y_norm", u)])
                    for kb in range(KB):
                        ins = pe.transpose(bank(e)[:, kb * P:(kb + 1) * P], y[:, u % Y_BUFS, kb * P:(kb + 1) * P],
                                           ident)
                    ins.then_inc(done, 1)
                if name == "gate":
                    u = e[1]
                    pe.wait_ge(gate_w_in, 16)
                    taken(pe, ("yT", u))
                    for kb in range(KB):
                        ins = pe.matmul(bank(e)[:, 0:D], yT[:, kb, :], gate_w[:, kb, :], start=(kb == 0),
                                        stop=(kb == KB - 1))
                    ins.then_inc(done, 1)
                if name == "thoughtT":
                    k = e[1]
                    src = thought_norm if k <= STEPS else thought
                    if k <= STEPS:
                        pe.wait_ge(c_normed, c_norm_n[("c_norm", k)])
                    else:
                        taken(pe, ("downT", STEPS - 1))
                    if k == 0:
                        taken(pe, ("vecT", 0))
                    for kb in range(KB):
                        ins = pe.transpose(bank(e)[:, kb * NB:(kb + 1) * NB], src[:, kb * P:(kb + 1) * P],
                                           ident[0:NB, 0:NB])
                    ins.then_inc(done, 1)
                if name in ("agg", "bc"):
                    taken(pe, ("thoughtT", 0 if name == "agg" else STEPS + 1))
                    w = agg_w if name == "agg" else bc_w
                    pe.wait_ge(agg_w_in if name == "agg" else bc_w_in, 16)
                    for kb in range(KB):
                        ins = pe.matmul(bank(e)[0:NB, 0:D], thoughtT[:, kb, :], w[:, kb, :], start=(kb == 0),
                                        stop=(kb == KB - 1))
                    ins.then_inc(done, 1)
                if name == "up":
                    pe.wait_ge(thought_parts_made, e[1] + 1)
                    if e[1] == 0:
                        pe.wait_ge(w_parts_made, W_CHUNKS)
                    for j in range(HB):
                        for n in range(KB * PARTS):
                            kb, i = n // PARTS, n % PARTS
                            ins = pe.matmul(bank(e)[:, j * PARTS * NB:(j + 1) * PARTS * NB],
                                            d1_parts[:, i, kb, j * P:(j + 1) * P], thoughtT_parts[:, kb, :],
                                            start=(n == 0), stop=(n == KB * PARTS - 1))
                    ins.then_inc(done, 1)
                if name == "down":
                    pe.wait_ge(hid_parts_made, e[1] + 1)
                    if e[1] == 0:
                        pe.wait_ge(w_parts_made, 2 * W_CHUNKS)
                    for kb in range(KB):
                        for n in range(HB * PARTS):
                            j, i = n // PARTS, n % PARTS
                            ins = pe.matmul(bank(e)[:, kb * PARTS * NB:(kb + 1) * PARTS * NB],
                                            d2_parts[:, i, j, kb * P:(kb + 1) * P], hid_parts[:, j, :],
                                            start=(n == 0), stop=(n == HB * PARTS - 1))
                    ins.then_inc(done, 1)
                if name == "downT":
                    taken(pe, ("down", e[1]))
                    for kb in range(KB):
                        ins = pe.transpose(bank(e)[0:NB, kb * P:(kb + 1) * P], down_sumT[:, kb, :], ident)
                    ins.then_inc(done, 1)
                if name == "bc_rows":
                    taken(pe, ("bc", 0))
                    pe.wait_ge(row_pick_in, 16)
                    for i in range(2):
                        ins = pe.matmul(bank(e)[:, i * D:(i + 1) * D], row_pick[:, 2 * e[1] + i, :], bc4[:, :],
                                        start=True, stop=True)
                    ins.then_inc(done, 1)


_INS = ["x", "ctx_512", "g_xattn", "g_ffn", "L0_xattn_Wq", "L0_xattn_w_kc_q", "L0_xattn_w_kc_kv", "L0_xattn_W_qr",
        "L0_xattn_W_kr", "L0_xattn_Wo", "L0_ffn_in_gamma", "L0_ffn_in_beta", "L0_ffn_agg_w", "L0_ffn_agg_b",
        "L0_ffn_pn_gamma", "L0_ffn_pn_beta", "L0_ffn_d1_w", "L0_ffn_d1_b", "L0_ffn_d2_w", "L0_ffn_d2_b",
        "L0_ffn_bc_w", "L0_ffn_bc_b", "L0_ffn_gate_w", "L0_ffn_gate_b", "L0_ffn_out_gamma", "L0_ffn_out_beta"]


def shape_constants():
    import numpy as np

    f = np.float32
    inv_freq = (f(1.0) / f(10000.0) ** (np.arange(0, DC, 2, dtype=f) / f(DC))).astype(f)
    angle = np.arange(S, dtype=f)[:, None] * inv_freq[None, :]
    sin = np.repeat(np.sin(angle), 2, axis=-1).astype(f)
    cos = np.repeat(np.cos(angle), 2, axis=-1).astype(f)
    sin[:, :DC // 2] *= f(-1.0)

    def by_partition(table):
        return table.reshape(LB, P, DC).transpose(1, 0, 2).reshape(P, LB * DC)

    consts = np.concatenate([np.eye(P, dtype=f), by_partition(cos), by_partition(sin)], axis=1)
    row_pick = np.repeat(np.eye(NB, dtype=f)[:, :, None], P, axis=2)
    return {"consts": np.ascontiguousarray(consts), "row_pick": np.ascontiguousarray(row_pick)}


def kernel(**inputs):
    import numpy as np
    import concourse.bacc as bacc
    from concourse.bass_utils import run_bass_kernel_spmd

    nc = bacc.Bacc("TRN2", target_bir_lowering=False, num_devices=1)
    arrays, aps = {}, {}
    given = {name: np.ascontiguousarray(inputs[name]) for name in _INS}
    for name, a in {**given, **shape_constants()}.items():
        arrays[f"in_{name}"] = a
        aps[name] = nc.dram_tensor(f"in_{name}", a.shape, mybir.dt.from_np(a.dtype), kind="ExternalInput").ap()
    out = nc.dram_tensor("out_x", (NB, S, D), F32, kind="ExternalOutput").ap()
    gated_cross_attention_ffn(nc, aps, out)
    r = run_bass_kernel_spmd(nc, [arrays], core_ids=[0])
    return r.results[0]["out_x"]
```
